# Optimizing a Trainium2 kernel written in Bass

```python
import numpy as np
import jax
import jax.numpy as jnp

def _softmax(x, axis=-1):
    return jax.nn.softmax(x, axis=axis)

def _gelu(x):
    return jax.nn.gelu(x, approximate=True)

def _silu(x):
    return jax.nn.silu(x)

def _sigmoid(x):
    return jax.nn.sigmoid(x)

def _layernorm(x, axis=-1, eps=1e-05):
    m = jnp.mean(x, axis=axis, keepdims=True)
    v = jnp.var(x, axis=axis, keepdims=True)
    return (x - m) / jnp.sqrt(v + eps)

def _scatter_add(tgt, idx, src, axis=0):
    return tgt.at[idx].add(src)

def _segment_sum(src, seg, n):
    return jax.ops.segment_sum(src, seg, n)
kernel_name = 'mk_adj_ffn_d1_adj_r2_ada487'

def setup_inputs(seed: int=0):
    np.random.seed(seed)
    _w = jnp.asarray

    def _rec_inputs():
        import jax
        import jax.numpy as jnp
        _gk = jax.random.key(seed)
        x = -0.001547 + 1.001 * jax.random.normal(jax.random.fold_in(_gk, 1), (128, 128, 256), jnp.float32)
        _a = jax.random.bernoulli(jax.random.fold_in(_gk, 2), 0.125, (128, 128))
        _a = jnp.logical_or(_a, jnp.swapaxes(_a, -1, -2))
        _a = jnp.logical_or(_a, jnp.eye(128, dtype=bool))
        _af = _a.astype(jnp.float32)
        _af = _af * jax.random.uniform(jax.random.fold_in(_gk, 3), (128, 128), jnp.float32, 0.05, 0.237401)
        adj = _af
        return (x, adj)
    x, adj = _rec_inputs()

    def _L0_gnn_setup():
        import jax, jax.numpy as jnp
        import numpy as np
        key = jax.random.key(seed)
        k1, k2, k3, k4 = jax.random.split(key, 4)
        B, D, N = (4, 128, 256)
        scale = 1.0 / np.sqrt(2 * D)
        x = jax.random.normal(k1, (B, D, N), dtype=jnp.float32)
        W1 = jax.random.normal(k2, (D, D), dtype=jnp.float32) * scale
        W2 = jax.random.normal(k3, (D, D), dtype=jnp.float32) * scale
        b = jax.random.normal(k4, (D,), dtype=jnp.float32) * scale
        return {'x': x, 'W1': W1, 'W2': W2, 'b': b}
    _L0_gnn_all = _L0_gnn_setup()
    _L0_gnn_in = {k: v for k, v in _L0_gnn_all.items() if k in ('b',)}
    del _L0_gnn_all

    def _L0_ffn_setup():
        import jax, jax.numpy as jnp
        import numpy as np
        E = 64
        K = 2
        D = 256
        H = 128
        NSH = 2
        ROUTE_SCALE = 2.5
        CAP = 512
        STD = 0.02
        key = jax.random.key(seed)
        ks = jax.random.split(key, 8)
        x = jax.random.normal(ks[0], (4, 1024, D), dtype=jnp.float32)
        gate_w = jax.random.normal(ks[1], (E, D), dtype=jnp.float32) * STD
        w1 = jax.random.normal(ks[2], (E, D, H), dtype=jnp.float32) * STD
        w3 = jax.random.normal(ks[3], (E, D, H), dtype=jnp.float32) * STD
        w2 = jax.random.normal(ks[4], (E, H, D), dtype=jnp.float32) * STD
        sw1 = jax.random.normal(ks[5], (D, H * NSH), dtype=jnp.float32) * STD
        sw3 = jax.random.normal(ks[6], (D, H * NSH), dtype=jnp.float32) * STD
        sw2 = jax.random.normal(ks[7], (H * NSH, D), dtype=jnp.float32) * STD
        return {'x': x, 'gate_w': gate_w, 'w1': w1, 'w3': w3, 'w2': w2, 'sw1': sw1, 'sw3': sw3, 'sw2': sw2}
    _L0_ffn_all = _L0_ffn_setup()
    _L0_ffn_in = {k: v for k, v in _L0_ffn_all.items() if k in ('gate_w', 'w1', 'w3', 'w2', 'sw1', 'sw3', 'sw2')}
    del _L0_ffn_all
    return {'x': x, 'adj': adj, 'L0_gnn_b': _L0_gnn_in['b'], 'L0_ffn_gate_w': _L0_ffn_in['gate_w'], 'L0_ffn_w1': _L0_ffn_in['w1'], 'L0_ffn_w3': _L0_ffn_in['w3'], 'L0_ffn_w2': _L0_ffn_in['w2'], 'L0_ffn_sw1': _L0_ffn_in['sw1'], 'L0_ffn_sw3': _L0_ffn_in['sw3'], 'L0_ffn_sw2': _L0_ffn_in['sw2']}

def reference(x, adj, L0_gnn_b, L0_ffn_gate_w, L0_ffn_w1, L0_ffn_w3, L0_ffn_w2, L0_ffn_sw1, L0_ffn_sw3, L0_ffn_sw2):
    import jax
    import jax.numpy as jnp

    def _L0_gnn_ref(x, W1, W2, b):
        import jax, jax.numpy as jnp
        import numpy as np
        A = jnp.einsum('od,bdn->bon', W1, x)
        C = jnp.einsum('od,bdn->bon', W2, x) + b[None, :, None]
        pre = A[:, :, None, :] + (C - A)[:, :, :, None]
        out = jnp.max(jax.nn.relu(pre), axis=-1)
        return out

    def _L0_ffn_ref(x, gate_w, w1, w3, w2, sw1, sw3, sw2):
        import jax, jax.numpy as jnp
        import numpy as np
        E = 64
        K = 2
        D = 256
        H = 128
        NSH = 2
        ROUTE_SCALE = 2.5
        CAP = 512
        STD = 0.02
        bs, slen, d = x.shape
        xf = x.reshape(-1, d)
        logits = xf @ gate_w.T
        scores = jax.nn.sigmoid(logits.astype(jnp.float32))
        top_scores, top_idx = jax.lax.top_k(scores, K)
        top_scores = top_scores / (top_scores.sum(-1, keepdims=True) + 1e-20)
        top_scores = top_scores * ROUTE_SCALE
        flat_e = top_idx.reshape(-1)
        x_pairs = jnp.repeat(xf, K, axis=0)
        oh = jax.nn.one_hot(flat_e, E, dtype=jnp.int32)
        pos = jnp.take_along_axis(jnp.cumsum(oh, axis=0), flat_e[:, None], axis=1)[:, 0] - 1
        buf = jnp.zeros((E, CAP, d), dtype=xf.dtype).at[flat_e, pos].set(x_pairs, mode='drop')
        h = jax.nn.silu(jnp.einsum('ecd,edh->ech', buf, w1)) * jnp.einsum('ecd,edh->ech', buf, w3)
        y = jnp.einsum('ech,ehd->ecd', h, w2)
        valid = (pos < CAP)[:, None]
        y_pairs = jnp.where(valid, y[flat_e, jnp.minimum(pos, CAP - 1)], 0.0)
        routed = (y_pairs.reshape(-1, K, d) * top_scores[..., None].astype(xf.dtype)).sum(axis=1)
        shared = jax.nn.silu(xf @ sw1) * (xf @ sw3) @ sw2
        return (shared + routed).reshape(bs, slen, d)
    x = x + _L0_gnn_ref(_layernorm(x, axis=-1), adj, adj, L0_gnn_b)
    x = x + _L0_ffn_ref(_layernorm(x, axis=-1), L0_ffn_gate_w, L0_ffn_w1, L0_ffn_w3, L0_ffn_w2, L0_ffn_sw1, L0_ffn_sw3, L0_ffn_sw2)
    return x

_drawn_inputs = setup_inputs


def setup_inputs(seed=0):
    import zlib

    import numpy as np

    out = dict(_drawn_inputs(seed))
    spreads = {}
    factors = {'L0_ffn_gate_w': 7.442,
     'L0_ffn_w1': 7.396,
     'L0_ffn_w3': 7.307,
     'L0_ffn_w2': 7.31,
     'L0_ffn_sw1': 8.0,
     'L0_ffn_sw3': 8.0,
     'L0_ffn_sw2': 8.0,
     'L0_gnn_b': 8.0}
    for name, (base, spread) in spreads.items():
        noise = np.random.default_rng([zlib.crc32(name.encode()), seed]).standard_normal(out[name].shape)
        drawn = base * np.exp(spread * noise) if base else spread * noise
        out[name] = jnp.asarray(drawn.astype(out[name].dtype))
    for name, factor in factors.items():
        out[name] = (out[name] * factor).astype(out[name].dtype)
    return out
```

```python
import concourse.bass as bass
from concourse import mybir
from contextlib import ExitStack


F32 = mybir.dt.float32
F32R = mybir.dt.float32r
BF16 = mybir.dt.bfloat16
FP16 = mybir.dt.float16
U32 = mybir.dt.uint32
ACT = mybir.ActivationFunctionType
ALU = mybir.AluOpType
AX = mybir.AxisListType

P = 128
CAP = 512
TOPK = 2
ROUTE_SCALE = 2.5
EPS = 1e-5
G = 4
REC = 7 * G


def run_three_stages(engine, step, pairs):
    step((0, 0), None, None)
    step((0, 1), (0, 0), None)
    step((1, 0), (0, 1), (0, 0))
    step((1, 1), (1, 0), (0, 1))
    with engine.Fori(1, pairs - 1) as j:
        step((j + 1, 0), (j, 1), (j, 0))
        step((j + 1, 1), (j + 1, 0), (j, 1))
    step(None, (pairs - 1, 1), (pairs - 1, 0))
    step(None, None, (pairs - 1, 1))


def run_pairs(engine, step, pairs):
    for q in range(2):
        step(0, q)
    with engine.Fori(1, pairs) as i:
        for q in range(2):
            step(i, q)


def wait_before(engine, sems, at, n):
    i, q = at
    if q == 1:
        engine.wait_ge(sems[0], (i + 1) * n)
    elif not (isinstance(i, int) and i == 0):
        engine.wait_ge(sems[1], i * n)


def wait_reuse(engine, sem, i, n):
    if not (isinstance(i, int) and i == 0):
        engine.wait_ge(sem, i * n)


def pass_waits(engine, passed):
    engine.sem_inc(passed, 1)


def build(nc, x, adj, b, gate_w, w1, w3, w2, sw1, sw3, sw2, out):
    B, D, N = x.shape
    E, _, H = w1.shape
    SH = sw1.shape[1] // P
    C = N // P
    S = CAP // P
    NG = B // G
    K2 = G * TOPK
    assert D == P and H == P and S == G and C == 2 and SH == 2 and 2 * E == P

    xn_dram = nc.dram_tensor("xn_rows", [B * D, N], F32, kind="Internal").ap()
    y_dram = nc.dram_tensor("slot_rows", [E * CAP, N], F32, kind="Internal").ap()

    ctx = ExitStack()
    with ctx:
        def sb(name, shape, dt):
            return ctx.enter_context(nc.sbuf_tensor(name, shape, dt))

        def sb2(name, shape, dt):
            return [sb(f"{name}{q}", shape, dt) for q in range(2)]

        def sem(name):
            return ctx.enter_context(nc.semaphore(name))

        def sem2(name):
            return [sem(f"{name}{q}") for q in range(2)]

        passed = {engine: sem(f"passed_{engine}") for engine in ("pool", "dve", "pe")}

        bank = [ctx.enter_context(nc.psum_tensor(f"bank{k}", [P, 512], F32)) for k in range(8)]

        ident = sb("ident", [P, P], F32)
        ones = sb("ones", [P, P], BF16)
        before = sb("before", [P, P], BF16)
        zero = sb("zero", [P, 512], BF16)
        slot_iota = sb("slot_iota", [P, CAP], FP16)
        expert_iota = sb("expert_iota", [P, E], F32)
        part_iota = sb("part_iota", [P, 1], F32)
        tile_iota = sb("tile_iota", [P, B], F32)
        minus_half = sb("minus_half", [P, G], F32)
        minus_one = sb("minus_one", [P, G], F32)
        eps = sb("eps", [P, G], F32)
        join = sb("join", [P, E], F32)
        adj_raw = sb("adj_raw", [P, P], F32)
        adjT = sb("adjT", [P, P], F32)
        gate_raw = sb("gate_raw", [E, N], F32)
        gateT = sb("gateT", [P, C, E], F32)
        bias = sb("bias", [P, 1], F32)
        rec_all = sb("rec_all", [P, NG, REC], F32)
        tok_all = sb("tok_all", [P, NG, 5, G], F32)
        slot_all = sb("slot_all", [P, NG, K2], U32)
        token_of = sb("token_of", [P, E, S], U32)

        x_in = sb2("x_in", [P, G, N], F32)
        xn = sb2("xn", [P, G, N], F32)
        xT_hi = sb2("xT_hi", [P, C, 512], F32R)
        xT_lo = sb2("xT_lo", [P, C, 512], F32R)
        work_a = sb2("work_a", [P, 4096], F32)
        work_b = sb2("work_b", [P, 2048], F32)

        stats = sb2("stats", [P, G, 6], F32)
        mv = sb2("mv", [P, G, 2], F32)
        var_eps = sb2("var_eps", [P, G], F32)
        norm = sb2("norm", [P, 2, G], F32)
        neg_rstd = sb2("neg_rstd", [P, G], F32)
        xT = [work_b[q][:, 0:C * 512].rearrange("p (c t) -> p c t", c=C) for q in range(2)]
        logitT = [work_b[q][0:E, C * 512:C * 512 + 512] for q in range(2)]
        score = [work_b[q][:, 1536:1536 + G * E].rearrange("p (t e) -> p t e", t=G) for q in range(2)]
        top8 = sb2("top8", [P, G, 8], F32)
        idx8 = sb2("idx8", [P, G, 8], U32)
        rec = sb2("rec", [P, REC], F32)
        onehot = sb2("onehot", [P, G, TOPK, E], BF16)
        mask = sb2("mask", [P, G, E], BF16)
        seen = sb2("seen", [P, G, E], BF16)
        tagged = sb2("tagged", [P, K2, 2, E], BF16)
        posdot = sb("posdot", [P, K2, E], F32)
        at_pos = [work_a[q][:, 0:2048].bitcast(BF16).rearrange("p (k s) -> p k s", k=K2) for q in range(2)]

        s_const = sem("s_const")
        s_raw = [sem(f"s_raw{k}") for k in range(3)]
        s_wT = sem("s_wT")
        s_wTc = sem("s_wTc")
        x_loaded = sem2("x_loaded")
        stats_done = sem2("stats_done")
        mv_done = sem2("mv_done")
        norm_step = sem2("norm_step")
        norm_saved = sem2("norm_saved")
        ln_done = sem2("ln_done")
        xn_stored = sem2("xn_stored")
        xnT_done = sem2("xnT_done")
        xT_done = sem2("xT_done")
        gate_done = sem2("gate_done")
        logitT_done = sem2("logitT_done")
        logit_done = sem2("logit_done")
        score_done = sem2("score_done")
        gnn_done = sem2("gnn_done")
        gmax_done = sem2("gmax_done")
        top_done = sem2("top_done")
        idx_done = sem2("idx_done")
        pick_done = sem2("pick_done")
        onehot_done = sem2("onehot_done")
        mask_done = sem2("mask_done")
        seen_done = sem2("seen_done")
        tagged_done = sem2("tagged_done")
        prefix_done = sem2("prefix_done")
        posdot_done = sem2("posdot_done")
        pos_done = sem2("pos_done")
        at_done = sem2("at_done")
        table_done = sem2("table_done")
        rec_saved = sem2("rec_saved")
        s_table = sem("s_table")
        s_tabc = sem("s_tabc")
        s_join = sem("s_join")
        s_fin = sem("s_fin")

        psT, psG, psA, psL, psP, psTab = bank[0:2], bank[2], bank[3:5], bank[5], bank[6], bank[7]

        with nc.Block() as block:
            @block.sync
            def _(sp):
                def load(i, q):
                    tile0 = (2 * i + q) * G
                    sp.dma_start(x_in[q][:], x[bass.ds(tile0, G)].rearrange("t d n -> d t n"))\
                        .then_inc(x_loaded[q], 16)

                def store(i, q):
                    sp.wait_ge(ln_done[q], G * (i + 1))
                    row0 = (2 * i + q) * G * D
                    sp.dma_start(xn_dram[bass.ds(row0, G * D)].rearrange("(t d) n -> d t n", t=G), xn[q][:])\
                        .then_inc(xn_stored[q], 16)

                sp.dma_start(adj_raw[:], adj).then_inc(s_raw[0], 16)
                load(0, 0)
                load(0, 1)
                sp.dma_start(gate_raw[:], gate_w).then_inc(s_raw[1], 16)
                sp.dma_start(bias[:], b.rearrange("(d a) -> d a", a=1)).then_inc(s_raw[2], 16)
                with sp.Fori(0, NG // 2 - 1) as i:
                    for q in range(2):
                        store(i, q)
                        load(i + 1, q)
                for q in range(2):
                    store(NG // 2 - 1, q)
                for q in range(2):
                    sp.wait_ge(xn_stored[q], 16 * (NG // 2))

            @block.gpsimd
            def _(pool):
                pool.memset(ident[:], 0.0).then_inc(s_const, 1)
                pool.memset(before[:], 1.0).then_inc(s_const, 1)
                pool.memset(join[:], 0.0).then_inc(s_const, 1)
                pool.memset(ones[:], 1.0).then_inc(s_const, 1)
                pool.memset(zero[:], 0.0).then_inc(s_const, 1)
                pool.memset(minus_half[:], -0.5).then_inc(s_const, 1)
                pool.memset(minus_one[:], -1.0).then_inc(s_const, 1)
                pool.memset(eps[:], EPS).then_inc(s_const, 1)
                pool.memset(seen[0][:, 0, :], 0.0).then_inc(s_const, 1)
                pool.iota(slot_iota[:], [[1, CAP]], base=0, channel_multiplier=0,
                          allow_small_or_imprecise_dtypes=True).then_inc(s_const, 1)
                pool.iota(expert_iota[:], [[1, E]], base=0, channel_multiplier=0,
                          allow_small_or_imprecise_dtypes=True).then_inc(s_const, 1)
                pool.iota(part_iota[:], [[0, 1]], base=0, channel_multiplier=1,
                          allow_small_or_imprecise_dtypes=True).then_inc(s_const, 1)
                pool.iota(tile_iota[:], [[1, B]], base=0, channel_multiplier=0,
                          allow_small_or_imprecise_dtypes=True).then_inc(s_const, 1)
                pool.wait_ge(s_const, 13)
                pool.affine_select(out=ident[:], in_=ident[:], compare_op=ALU.not_equal, fill=1.0, base=0,
                                   pattern=[[-1, P]], channel_multiplier=1).then_inc(s_const, 1)
                pool.affine_select(out=before[:], in_=before[:], compare_op=ALU.is_gt, fill=0.0, base=0,
                                   pattern=[[1, P]], channel_multiplier=-1).then_inc(s_const, 1)
                pool.affine_select(out=join[:], in_=join[:], compare_op=ALU.not_equal, fill=1.0, base=0,
                                   pattern=[[-1, E]], channel_multiplier=1).then_inc(s_const, 1)
                pool.wait_ge(s_const, 16)
                pool.affine_select(out=join[:], in_=join[:], compare_op=ALU.not_equal, fill=float(P), base=-E,
                                   pattern=[[-1, E]], channel_multiplier=1).then_inc(s_const, 1)

                def step(a, bb, c):
                    if a:
                        i, q = a
                        pool.wait_ge(mv_done[q], G * (i + 1))
                        wait_reuse(pool, ln_done[q], i, G)
                        pool.tensor_tensor(var_eps[q][:], mv[q][:, :, 1], eps[:], ALU.add)\
                            .then_inc(norm_step[q], 1)
                        pool.wait_ge(norm_step[q], 4 * i + 1)
                        pool.tensor_tensor(norm[q][:, 0, :], var_eps[q][:], minus_half[:], ALU.pow)\
                            .then_inc(norm_step[q], 1)
                        pool.wait_ge(norm_step[q], 4 * i + 2)
                        pool.tensor_tensor(neg_rstd[q][:], norm[q][:, 0, :], minus_one[:], ALU.mult)\
                            .then_inc(norm_step[q], 1)
                        pool.wait_ge(norm_step[q], 4 * i + 3)
                        pool.tensor_tensor(norm[q][:, 1, :], neg_rstd[q][:], mv[q][:, :, 0], ALU.mult)\
                            .then_inc(norm_step[q], 1)
                    if bb:
                        i, q = bb
                        oh = onehot[q][:].rearrange("p t k e -> p (t k) e")
                        pool.wait_ge(onehot_done[q], i + 1)
                        wait_reuse(pool, prefix_done[q], i, 1)
                        pool.tensor_tensor(mask[q][:], onehot[q][:, :, 0, :], onehot[q][:, :, 1, :], ALU.add)\
                            .then_inc(mask_done[q], 1)
                        pool.wait_ge(mask_done[q], i + 1)
                        for t in range(1, G):
                            pool.tensor_tensor(seen[q][:, t, :], seen[q][:, t - 1, :], mask[q][:, t - 1, :],
                                               ALU.add).then_inc(seen_done[q], 1)
                            pool.wait_ge(seen_done[q], G * i + t)
                        wait_before(pool, prefix_done, bb, 1)
                        pool.tensor_tensor(seen[1 - q][:, 0, :], seen[q][:, G - 1, :], mask[q][:, G - 1, :],
                                           ALU.add).then_inc(seen_done[q], 1)
                        wait_reuse(pool, table_done[q], i, 1)
                        pass_waits(pool, passed["pool"])
                        pool.tensor_scalar(tagged[q][:, :, 0, :], oh, part_iota[:, 0:1], None, ALU.mult)\
                            .then_inc(tagged_done[q], 1)
                        group = 2 * i + q
                        pool.tensor_tensor(
                            tagged[q][:, :, 1, :].rearrange("p (t k) e -> p t k e", k=TOPK), onehot[q][:],
                            tile_iota[:, bass.ds(group * G, G)].unsqueeze(2).unsqueeze(3)
                            .to_broadcast([P, G, TOPK, E]), ALU.mult).then_inc(tagged_done[q], 1)
                        pool.wait_ge(seen_done[q], G * (i + 1))
                    if a:
                        i, q = a
                        pool.wait_ge(norm_step[q], 4 * i + 4)
                        pool.tensor_copy(tok_all[:, 2 * i + q, 0:2, :], norm[q][:]).then_inc(norm_saved[q], 1)
                    if c:
                        i, q = c
                        pool.wait_ge(pos_done[q], i + 1)
                        pool.wait_ge(gmax_done[q], G // 2 * (i + 1))
                        pool.tensor_copy(rec_all[:, 2 * i + q, :], rec[q][:]).then_inc(rec_saved[q], 1)

                run_three_stages(pool, step, NG // 2)

            @block.scalar
            def _(act):
                def step(a, bb, c):
                    if a:
                        i, q = a
                        act.wait_ge(norm_step[q], 4 * (i + 1))
                        act.wait_ge(x_loaded[q], 16 * (i + 1))
                        wait_reuse(act, xn_stored[q], i, 16)
                        wait_reuse(act, gnn_done[q], i, G // 2)
                        for t in range(G):
                            act.activation(xn[q][:, t, :], x_in[q][:, t, :], ACT.Identity,
                                           bias=norm[q][:, 1, t:t + 1], scale=norm[q][:, 0, t:t + 1])\
                                .then_inc(ln_done[q], 1)
                        wait_reuse(act, gate_done[q], i, 1)
                        for ch in range(C):
                            act.wait_ge(xnT_done[q], C * i + ch + 1)
                            act.activation(xT[q][:, ch, :], psT[ch][:], ACT.Copy).then_inc(xT_done[q], 1)
                        act.wait_ge(gate_done[q], i + 1)
                        wait_reuse(act, logit_done[q], i, 1)
                        act.activation(logitT[q], psG[0:E, :], ACT.Copy).then_inc(logitT_done[q], 1)
                        act.wait_ge(logit_done[q], i + 1)
                        wait_reuse(act, idx_done[q], i, G)
                        act.activation(score[q], psL[:, 0:G * E].rearrange("p (t e) -> p t e", t=G),
                                       ACT.Sigmoid).then_inc(score_done[q], 1)

                run_three_stages(act, step, NG // 2)
                act.wait_ge(s_table, 1)
                wait_before(act, at_done, (NG // 2, 0), K2)
                act.activation(work_a[0][:, 0:512], psTab[:], ACT.Copy).then_inc(s_tabc, 1)

            @block.vector
            def _(dve):
                dve.wait_ge(s_wT, 2)
                dve.tensor_copy(adjT[:], psA[0][:, 0:P]).then_inc(s_wTc, 1)
                dve.tensor_copy(gateT[:].rearrange("p c e -> p (c e)"), psA[1][:, 0:C * E]).then_inc(s_wTc, 1)

                def step(a, bb, c):
                    if a:
                        i, q = a
                        dve.wait_ge(x_loaded[q], 16 * (i + 1))
                        for t in range(G):
                            dve.bn_stats(stats[q][:, t, :], x_in[q][:, t, :]).then_inc(stats_done[q], 1)
                        wait_reuse(dve, norm_step[q], i, 4)
                        dve.wait_ge(stats_done[q], G * (i + 1))
                        pass_waits(dve, passed["dve"])
                        for t in range(G):
                            dve.bn_aggr(mv[q][:, t, :], stats[q][:, t, :]).then_inc(mv_done[q], 1)
                    if bb:
                        i, q = bb
                        dve.wait_ge(score_done[q], i + 1)
                        wait_reuse(dve, pick_done[q], i, 2)
                        pass_waits(dve, passed["dve"])
                        for t in range(G):
                            dve.max(top8[q][:, t, :], score[q][:, t, :]).then_inc(top_done[q], 1)
                        wait_reuse(dve, rec_saved[q], i, 1)
                        dve.wait_ge(top_done[q], G * (i + 1))
                        dve.tensor_copy(rec[q][:, 0:K2].rearrange("p (t k) -> p t k", k=TOPK),
                                        top8[q][:, :, 0:TOPK]).then_inc(pick_done[q], 1)
                        for t in range(G):
                            dve.max_index(idx8[q][:, t, :], top8[q][:, t, :], score[q][:, t, :])\
                                .then_inc(idx_done[q], 1)
                        dve.wait_ge(idx_done[q], G * (i + 1))
                        dve.tensor_copy(rec[q][:, K2:2 * K2].rearrange("p (t k) -> p t k", k=TOPK),
                                        idx8[q][:, :, 0:TOPK]).then_inc(pick_done[q], 1)
                        dve.wait_ge(pick_done[q], 2 * (i + 1))
                        wait_reuse(dve, tagged_done[q], i, 2)
                        dve.tensor_tensor(onehot[q][:].rearrange("p t k e -> p (t k) e"),
                                          rec[q][:, K2:2 * K2].unsqueeze(2).to_broadcast([P, K2, E]),
                                          expert_iota[:].unsqueeze(1).to_broadcast([P, K2, E]),
                                          ALU.is_equal).then_inc(onehot_done[q], 1)
                    if c:
                        i, q = c
                        dve.wait_ge(prefix_done[q], i + 1)
                        dve.wait_ge(onehot_done[q], i + 1)
                        wait_before(dve, pos_done, c, 1)
                        dve.tensor_tensor(
                            posdot[:].rearrange("p (t k) e -> p t k e", k=TOPK), onehot[q][:],
                            psP[:, 0:G * E].rearrange("p (t e) -> p t e", t=G).unsqueeze(2)
                            .to_broadcast([P, G, TOPK, E]), ALU.mult).then_inc(posdot_done[q], 1)
                        dve.wait_ge(posdot_done[q], i + 1)
                        dve.reduce_sum(rec[q][:, 2 * K2:3 * K2], posdot[:], AX.X).then_inc(pos_done[q], 1)
                        dve.wait_ge(pos_done[q], i + 1)
                        wait_reuse(dve, table_done[q], i, 1)
                        for k in range(K2):
                            dve.tensor_scalar(at_pos[q][:, k, :], slot_iota[:],
                                              rec[q][:, 2 * K2 + k:2 * K2 + k + 1], None, ALU.is_equal)\
                                .then_inc(at_done[q], 1)
                    if bb:
                        i, q = bb
                        for j in range(G // 2):
                            dve.wait_ge(gnn_done[q], G // 2 * i + j + 1)
                            dve.reduce_max(rec[q][:, 3 * K2 + 2 * j:3 * K2 + 2 * j + 2],
                                           psA[j][:].rearrange("p (t n) -> p t n", t=2), AX.X)\
                                .then_inc(gmax_done[q], 1)

                dve.wait_ge(s_const, 17)
                run_three_stages(dve, step, NG // 2)

                for q in range(2):
                    dve.wait_ge(rec_saved[q], NG // 2)
                    dve.wait_ge(norm_saved[q], NG // 2)
                dve.wait_ge(s_raw[2], 16)
                fin = [0]

                def after(ins):
                    fin[0] += 1
                    ins.then_inc(s_fin, 1)
                    dve.wait_ge(s_fin, fin[0])

                for q in range(2):
                    dve.wait_ge(table_done[q], NG // 2)
                fa = work_a[1]
                total = fa[:, 0:B].rearrange("p (g t) -> p g t", t=G)
                kept = fa[:, B:3 * B].rearrange("p (g k) -> p g k", k=K2)
                scaled = fa[:, 3 * B:5 * B].rearrange("p (g k) -> p g k", k=K2)
                clipped = fa[:, 5 * B:7 * B].rearrange("p (g k) -> p g k", k=K2)
                rmax = fa[:, 7 * B:8 * B].rearrange("p (g t) -> p g t", t=G)
                s_of = rec_all[:, :, 0:K2].rearrange("p g (t k) -> p g t k", k=TOPK)
                pos_of = rec_all[:, :, 2 * K2:3 * K2]
                after(dve.tensor_tensor(total, s_of[:, :, :, 0], s_of[:, :, :, 1], ALU.add))
                after(dve.tensor_scalar(total, total, 1e-20, None, ALU.add))
                after(dve.reciprocal(total, total))
                after(dve.tensor_scalar(kept, pos_of, float(CAP), ROUTE_SCALE, ALU.is_lt, ALU.mult))
                after(dve.tensor_tensor(scaled, kept, rec_all[:, :, 0:K2], ALU.mult))
                sc4 = scaled.rearrange("p g (t k) -> p g t k", k=TOPK)
                for k in range(TOPK):
                    after(dve.tensor_tensor(tok_all[:, :, 3 + k, :], sc4[:, :, :, k], total, ALU.mult))
                after(dve.tensor_scalar(clipped, pos_of, float(CAP - 1), None, ALU.min))
                after(dve.scalar_tensor_tensor(slot_all[:], rec_all[:, :, K2:2 * K2], float(CAP), clipped,
                                               ALU.mult, ALU.add))
                after(dve.tensor_scalar(tok_all[:, :, 2, :], rec_all[:, :, 3 * K2:3 * K2 + G], bias[:, 0:1], 0.0,
                                        ALU.add, ALU.max))
                dve.wait_ge(s_join, 1)
                dve.tensor_copy(token_of[:].rearrange("p e s -> p s e"),
                                psA[0][:, 0:S * E].rearrange("p (s e) -> p s e", s=S))

            @block.tensor
            def _(pe):
                pe.wait_ge(s_const, 17)
                pe.wait_ge(s_raw[0], 16)
                pe.transpose(psA[0][:, 0:P], adj_raw[:], ident[:]).then_inc(s_wT, 1)
                pe.wait_ge(s_raw[1], 16)
                for ch in range(C):
                    last = pe.transpose(psA[1][:, ch * E:(ch + 1) * E], gate_raw[:, ch::C], ident[0:E, 0:E])
                last.then_inc(s_wT, 1)
                pe.matmul(psTab[:], zero[:, 0:P], zero[:], start=True, stop=False)
                pe.wait_ge(s_wTc, 2)

                def step(a, bb, c):
                    if a:
                        i, q = a
                        pe.wait_ge(ln_done[q], G * (i + 1))
                        wait_before(pe, xT_done, a, C)
                        for ch in range(C):
                            for t in range(G):
                                last = pe.transpose(psT[ch][:, t * P:(t + 1) * P], xn[q][:, t, ch::C], ident[:])
                            last.then_inc(xnT_done[q], 1)
                        wait_before(pe, gmax_done, a, G // 2)
                        for j in range(G // 2):
                            pe.matmul(psA[j][:], adjT[:],
                                      xn[q][:, 2 * j:2 * j + 2, :].rearrange("p t n -> p (t n)"),
                                      start=True, stop=True).then_inc(gnn_done[q], 1)
                        pe.wait_ge(xT_done[q], C * (i + 1))
                        wait_before(pe, logitT_done, a, 1)
                        for ch in range(C):
                            last = pe.matmul(psG[0:E, :], gateT[:, ch, :], xT[q][:, ch, :],
                                             start=(ch == 0), stop=(ch == C - 1))
                        last.then_inc(gate_done[q], 1)
                    if c:
                        i, q = c
                        pe.wait_ge(at_done[q], K2 * (i + 1))
                        pe.wait_ge(tagged_done[q], 2 * (i + 1))
                        for k in range(K2):
                            last = pe.matmul(psTab[:], tagged[q][:, k].rearrange("p a e -> p (a e)"),
                                             at_pos[q][:, k, :], start=False, stop=False)
                        last.then_inc(table_done[q], 1)
                    if a:
                        i, q = a
                        pe.wait_ge(logitT_done[q], i + 1)
                        wait_before(pe, score_done, a, 1)
                        pass_waits(pe, passed["pe"])
                        for t in range(G):
                            last = pe.transpose(psL[:, t * E:(t + 1) * E], logitT[q][:, t * P:(t + 1) * P],
                                                ident[0:E, 0:E])
                        last.then_inc(logit_done[q], 1)
                    if bb:
                        i, q = bb
                        pe.wait_ge(seen_done[q], G * i + G - 1)
                        wait_before(pe, seen_done, bb, G)
                        wait_before(pe, posdot_done, bb, 1)
                        pe.matmul(psP[:, 0:G * E], before[:], mask[q][:].rearrange("p t e -> p (t e)"),
                                  start=True, stop=False)
                        pe.matmul(psP[:, 0:G * E], ones[:], seen[q][:].rearrange("p t e -> p (t e)"),
                                  start=False, stop=True).then_inc(prefix_done[q], 1)

                run_three_stages(pe, step, NG // 2)
                pe.matmul(psTab[:], zero[:, 0:P], zero[:], start=False, stop=True).then_inc(s_table, 1)
                pe.wait_ge(s_tabc, 1)
                for q in range(2):
                    pe.wait_ge(gmax_done[q], G // 2 * (NG // 2))
                for s in range(S):
                    last = pe.matmul(psA[0][:, s * E:(s + 1) * E], work_a[0][:, s:512:S], join[:],
                                     start=True, stop=True)
                last.then_inc(s_join, 1)

        w13_raw = [work_a[q][:, 0:512].rearrange("p (w c h) -> p w c h", w=2, c=C) for q in range(2)]
        w2_raw = [work_a[q][:, 512:768] for q in range(2)]
        w13_hi = sb2("w13_hi", [P, 2, C, H], F32R)
        w13_lo = sb2("w13_lo", [P, 2, C, H], F32R)
        w2_hi = sb2("w2_hi", [P, N], F32R)
        w2_lo = sb2("w2_lo", [P, N], F32R)
        rows = xn
        token_now = sb2("token_now", [P, S], U32)
        silu = [work_b[q][:, 0:512] for q in range(2)]
        hid = [work_b[q][:, 512:1024] for q in range(2)]
        h_hi = sb2("h_hi", [P, SH, 512], F32R)
        h_lo = sb2("h_lo", [P, SH, 512], F32R)
        y_out = x_in

        w13_loaded = sem2("w13_loaded")
        w2_loaded = sem2("w2_loaded")
        w13_hi_done = sem2("w13_hi_done")
        w13_lo_done = sem2("w13_lo_done")
        w2_hi_done = sem2("w2_hi_done")
        w2_lo_done = sem2("w2_lo_done")
        token_set = sem2("token_set")
        gathered = sem2("gathered")
        rowsT_done = sem2("rowsT_done")
        rT_hi_done = sem2("rT_hi_done")
        rT_lo_done = sem2("rT_lo_done")
        g_done = sem2("g_done")
        u_done = sem2("u_done")
        silu_done = sem2("silu_done")
        hid_done = sem2("hid_done")
        h_hi_done = sem2("h_hi_done")
        h_lo_done = sem2("h_lo_done")
        y_done = sem2("y_done")
        y_act = sem2("y_act")
        y_dve = sem2("y_dve")
        y_stored = sem2("y_stored")

        def three_passes(pe, ps, terms):
            products = [(wv, mv_) for (w_hi, w_lo), (m_hi, m_lo) in terms
                        for wv, mv_ in ((w_hi, m_hi), (w_hi, m_lo), (w_lo, m_hi))]
            for n, (wv, mv_) in enumerate(products):
                last = pe.matmul(ps, wv, mv_, start=(n == 0), stop=(n == len(products) - 1))
            return last

        psT, psGU, psY = bank[0:2], [bank[2:4], bank[4:6]], bank[6:8]

        with nc.Block() as block:
            @block.sync
            def _(sp):
                def load(i, q):
                    e = 2 * i + q
                    wait_reuse(sp, w13_lo_done[q], i, 1)
                    wait_reuse(sp, w13_hi_done[q], i, 1)
                    for k, w in enumerate((w1, w3)):
                        sp.dma_start(w13_raw[q][:, k].rearrange("p c h -> p (c h)"),
                                     w[e].rearrange("(p c) h -> p (c h)", c=C)).then_inc(w13_loaded[q], 16)
                    wait_reuse(sp, w2_lo_done[q], i, 1)
                    wait_reuse(sp, w2_hi_done[q], i, 1)
                    sp.dma_start(w2_raw[q], w2[e]).then_inc(w2_loaded[q], 16)

                def store(i, q):
                    sp.wait_ge(y_act[q], i + 1)
                    sp.wait_ge(y_dve[q], i + 1)
                    row0 = (2 * i + q) * CAP
                    sp.dma_start(y_dram[bass.ds(row0, CAP)].rearrange("(p s) n -> p (s n)", s=S),
                                 y_out[q][:].rearrange("p s n -> p (s n)")).then_inc(y_stored[q], 16)

                load(0, 0)
                load(0, 1)
                with sp.Fori(0, E // 2 - 1) as i:
                    for q in range(2):
                        load(i + 1, q)
                        store(i, q)
                for q in range(2):
                    store(E // 2 - 1, q)
                for q in range(2):
                    sp.wait_ge(y_stored[q], 16 * (E // 2))

            @block.gpsimd
            def _(pool):
                def step(i, q):
                    wait_reuse(pool, gathered[q], i, 16 * S)
                    pool.tensor_copy(token_now[q][:], token_of[:, 2 * i + q, :]).then_inc(token_set[q], 1)
                    pool.wait_ge(token_set[q], i + 1)
                    wait_reuse(pool, rowsT_done[q], i, C)
                    pass_waits(pool, passed["pool"])
                    for s in range(S):
                        pool.indirect_dma_start(
                            out=rows[q][:, s, :], out_offset=None, in_=xn_dram,
                            in_offset=bass.IndirectOffsetOnAxis(ap=token_now[q][:, s:s + 1], axis=0))\
                            .then_inc(gathered[q], 16)

                run_pairs(pool, step, E // 2)

            @block.tensor
            def _(pe):
                def step(a, bb, c):
                    if a:
                        i, q = a
                        pe.wait_ge(gathered[q], 16 * S * (i + 1))
                        wait_before(pe, rT_hi_done, a, C)
                        wait_before(pe, rT_lo_done, a, C)
                        for ch in range(C):
                            for s in range(S):
                                last = pe.transpose(psT[ch][:, s * P:(s + 1) * P], rows[q][:, s, ch::C], ident[:])
                            last.then_inc(rowsT_done[q], 1)
                    if bb:
                        i, q = bb
                        pe.wait_ge(w13_hi_done[q], i + 1)
                        pe.wait_ge(w13_lo_done[q], i + 1)
                        pe.wait_ge(rT_hi_done[q], C * (i + 1))
                        pe.wait_ge(rT_lo_done[q], C * (i + 1))
                        wait_reuse(pe, silu_done[q], i, 1)
                        wait_reuse(pe, hid_done[q], i, 1)
                        for k, done in enumerate((g_done, u_done)):
                            three_passes(pe, psGU[q][k][:], [
                                ((w13_hi[q][:, k, ch], w13_lo[q][:, k, ch]), (xT_hi[q][:, ch], xT_lo[q][:, ch]))
                                for ch in range(C)]).then_inc(done[q], 1)
                    if c:
                        i, q = c
                        pe.wait_ge(w2_hi_done[q], i + 1)
                        pe.wait_ge(w2_lo_done[q], i + 1)
                        pe.wait_ge(h_hi_done[q], i + 1)
                        pe.wait_ge(h_lo_done[q], i + 1)
                        wait_before(pe, y_act, c, 1)
                        wait_before(pe, y_dve, c, 1)
                        for j in range(2):
                            for s in (2 * j, 2 * j + 1):
                                last = three_passes(pe, psY[j][:, s % 2 * N:(s % 2 + 1) * N], [
                                    ((h_hi[q][:, 0, s * P:(s + 1) * P], h_lo[q][:, 0, s * P:(s + 1) * P]),
                                     (w2_hi[q][:], w2_lo[q][:]))])
                            last.then_inc(y_done[q], 1)

                run_three_stages(pe, step, E // 2)

            @block.scalar
            def _(act):
                def step(a, bb, c):
                    if bb:
                        i, q = bb
                        act.wait_ge(g_done[q], i + 1)
                        wait_reuse(act, hid_done[q], i, 1)
                        act.activation(silu[q], psGU[q][0][:], ACT.Silu).then_inc(silu_done[q], 1)
                    if a:
                        i, q = a
                        wait_reuse(act, u_done[q], i, 1)
                        for ch in range(C):
                            act.wait_ge(rowsT_done[q], C * i + ch + 1)
                            act.activation(xT_hi[q][:, ch], psT[ch][:], ACT.Copy).then_inc(rT_hi_done[q], 1)
                        act.wait_ge(w13_loaded[q], 32 * (i + 1))
                        act.activation(w13_hi[q][:], w13_raw[q], ACT.Copy).then_inc(w13_hi_done[q], 1)
                    if bb:
                        i, q = bb
                        act.wait_ge(hid_done[q], i + 1)
                        wait_reuse(act, y_done[q], i, 2)
                        act.activation(h_hi[q][:, 0], hid[q], ACT.Copy).then_inc(h_hi_done[q], 1)
                        act.wait_ge(w2_loaded[q], 16 * (i + 1))
                        act.activation(w2_hi[q][:], w2_raw[q], ACT.Copy).then_inc(w2_hi_done[q], 1)
                    if c:
                        i, q = c
                        act.wait_ge(y_done[q], 2 * i + 1)
                        wait_reuse(act, y_stored[q], i, 16)
                        act.activation(y_out[q][:, 0:2, :].rearrange("p s n -> p (s n)"), psY[0][:], ACT.Copy)\
                            .then_inc(y_act[q], 1)

                run_three_stages(act, step, E // 2)

            @block.vector
            def _(dve):
                def step(a, bb, c):
                    if bb:
                        i, q = bb
                        dve.wait_ge(silu_done[q], i + 1)
                        dve.wait_ge(u_done[q], i + 1)
                        wait_reuse(dve, h_hi_done[q], i, 1)
                        wait_reuse(dve, h_lo_done[q], i, 1)
                        dve.tensor_tensor(hid[q], silu[q], psGU[q][1][:], ALU.mult).then_inc(hid_done[q], 1)
                    if a:
                        i, q = a
                        wait_reuse(dve, u_done[q], i, 1)
                        for ch in range(C):
                            dve.wait_ge(rT_hi_done[q], C * i + ch + 1)
                            dve.tensor_tensor(xT_lo[q][:, ch], psT[ch][:], xT_hi[q][:, ch].bitcast(F32),
                                              ALU.subtract).then_inc(rT_lo_done[q], 1)
                        dve.wait_ge(w13_hi_done[q], i + 1)
                        dve.tensor_tensor(w13_lo[q][:], w13_raw[q], w13_hi[q][:].bitcast(F32), ALU.subtract)\
                            .then_inc(w13_lo_done[q], 1)
                    if bb:
                        i, q = bb
                        dve.wait_ge(h_hi_done[q], i + 1)
                        wait_reuse(dve, y_done[q], i, 2)
                        dve.tensor_tensor(h_lo[q][:, 0], hid[q], h_hi[q][:, 0].bitcast(F32), ALU.subtract)\
                            .then_inc(h_lo_done[q], 1)
                        dve.wait_ge(w2_hi_done[q], i + 1)
                        dve.tensor_tensor(w2_lo[q][:], w2_raw[q], w2_hi[q][:].bitcast(F32), ALU.subtract)\
                            .then_inc(w2_lo_done[q], 1)
                    if c:
                        i, q = c
                        dve.wait_ge(y_done[q], 2 * (i + 1))
                        wait_reuse(dve, y_stored[q], i, 16)
                        dve.tensor_copy(y_out[q][:, 2:4, :].rearrange("p s n -> p (s n)"), psY[1][:])\
                            .then_inc(y_dve[q], 1)

                run_three_stages(dve, step, E // 2)

        sw13_hi = sb("sw13_hi", [P, 2, C, SH, P], F32R)
        sw13_lo = sb("sw13_lo", [P, 2, C, SH, P], F32R)
        sw2_hi = sb("sw2_hi", [P, SH, N], F32R)
        sw2_lo = sb("sw2_lo", [P, SH, N], F32R)
        sw13_raw = work_b[0][:, 0:1024].rearrange("p (w c s h) -> p w c s h", w=2, c=C, s=SH)
        sw2_raw = work_b[0][:, 1024:1536].rearrange("p (s n) -> p s n", s=SH)
        pair_rows = [work_a[q][:, 0:K2 * N].rearrange("p (k n) -> p k n", k=K2) for q in range(2)]
        slot_now = sb2("slot_now", [P, K2], U32)
        tok_now = sb2("tok_now", [P, 5, G], F32)
        res = sb2("res", [P, G, N], F32)
        s_silu = [work_b[q][:, 0:1024].rearrange("p (s t) -> p s t", s=SH) for q in range(2)]
        s_hid = [work_b[q][:, 1024:2048].rearrange("p (s t) -> p s t", s=SH) for q in range(2)]

        sw_loaded = sem("sw_loaded")
        sw_hi_done = sem("sw_hi_done")
        sw_lo_done = sem("sw_lo_done")
        x2_loaded = sem2("x2_loaded")
        now_set = sem2("now_set")
        pair_gathered = sem2("pair_gathered")
        ln2_done = sem2("ln2_done")
        x2T_done = sem2("x2T_done")
        x2T_hi = sem2("x2T_hi")
        x2T_lo = sem2("x2T_lo")
        sg_done = sem2("sg_done")
        su_done = sem2("su_done")
        ssilu_done = sem2("ssilu_done")
        shid_done = sem2("shid_done")
        sh_hi_done = sem2("sh_hi_done")
        sh_lo_done = sem2("sh_lo_done")
        sy_done = sem2("sy_done")
        base_done = sem2("base_done")
        one_done = sem2("one_done")
        res_done = sem2("res_done")
        res_loaded = sem2("res_loaded")
        out_stored = sem2("out_stored")

        psT, psS, psY = bank[0:2], [bank[2:4], bank[4:6]], bank[6:8]

        with nc.Block() as block:
            @block.sync
            def _(sp):
                def load(i, q):
                    tile0 = (2 * i + q) * G
                    wait_reuse(sp, ln2_done[q], i, G)
                    sp.dma_start(x_in[q][:], x[bass.ds(tile0, G)].rearrange("t d n -> d t n"))\
                        .then_inc(x2_loaded[q], 16)

                def load_residual(i, q):
                    tile0 = (2 * i + q) * G
                    wait_reuse(sp, out_stored[q], i, 16)
                    sp.dma_start(res[q][:], x[bass.ds(tile0, G)].rearrange("t d n -> d t n"))\
                        .then_inc(res_loaded[q], 16)

                def store(i, q):
                    tile0 = (2 * i + q) * G
                    sp.wait_ge(res_done[q], G * (i + 1))
                    sp.dma_start(out[bass.ds(tile0, G)].rearrange("t d n -> d t n"), res[q][:])\
                        .then_inc(out_stored[q], 16)

                for k, w in enumerate((sw1, sw3)):
                    sp.dma_start(sw13_raw[:, k].rearrange("p c s h -> p (c s h)"),
                                 w.rearrange("(p c) h -> p (c h)", c=C)).then_inc(sw_loaded, 16)
                sp.dma_start(sw2_raw, sw2.rearrange("(s p) n -> p s n", s=SH)).then_inc(sw_loaded, 16)
                for q in range(2):
                    load(0, q)
                    load_residual(0, q)
                with sp.Fori(0, NG // 2 - 1) as i:
                    for q in range(2):
                        load(i + 1, q)
                        store(i, q)
                        load_residual(i + 1, q)
                for q in range(2):
                    store(NG // 2 - 1, q)
                for q in range(2):
                    sp.wait_ge(out_stored[q], 16 * (NG // 2))

            @block.gpsimd
            def _(pool):
                def step(i, q):
                    wait_reuse(pool, pair_gathered[q], i, 16 * K2)
                    wait_reuse(pool, res_done[q], i, G)
                    pool.tensor_copy(slot_now[q][:], slot_all[:, 2 * i + q, :]).then_inc(now_set[q], 1)
                    pool.tensor_copy(tok_now[q][:], tok_all[:, 2 * i + q]).then_inc(now_set[q], 1)
                    pool.wait_ge(now_set[q], 2 * (i + 1))
                    pass_waits(pool, passed["pool"])
                    for k in range(K2):
                        pool.indirect_dma_start(
                            out=pair_rows[q][:, k, :], out_offset=None, in_=y_dram,
                            in_offset=bass.IndirectOffsetOnAxis(ap=slot_now[q][:, k:k + 1], axis=0))\
                            .then_inc(pair_gathered[q], 16)

                run_pairs(pool, step, NG // 2)

            @block.scalar
            def _(act):
                act.wait_ge(sw_loaded, 48)
                act.activation(sw13_hi[:].rearrange("p w c s h -> p (w c s h)"), work_b[0][:, 0:1024], ACT.Copy)\
                    .then_inc(sw_hi_done, 1)
                act.activation(sw2_hi[:], sw2_raw, ACT.Copy).then_inc(sw_hi_done, 1)

                def step(a, bb, c):
                    if a:
                        i, q = a
                        act.wait_ge(x2_loaded[q], 16 * (i + 1))
                        wait_reuse(act, x2T_done[q], i, C)
                        for t in range(G):
                            act.activation(xn[q][:, t, :], x_in[q][:, t, :], ACT.Identity,
                                           bias=tok_all[:, 2 * i + q, 1, t:t + 1],
                                           scale=tok_all[:, 2 * i + q, 0, t:t + 1])\
                                .then_inc(ln2_done[q], 1)
                    if bb:
                        i, q = bb
                        act.wait_ge(sw_lo_done, 2)
                        wait_reuse(act, shid_done[q], i, SH)
                        for s in range(SH):
                            act.wait_ge(sg_done[q], SH * i + s + 1)
                            act.activation(s_silu[q][:, s, :], psS[s][0][:], ACT.Silu).then_inc(ssilu_done[q], 1)
                    if a:
                        i, q = a
                        wait_reuse(act, su_done[q], i, SH)
                        for ch in range(C):
                            act.wait_ge(x2T_done[q], C * i + ch + 1)
                            act.activation(xT_hi[q][:, ch], psT[ch][:], ACT.Copy).then_inc(x2T_hi[q], 1)
                    if bb:
                        i, q = bb
                        wait_reuse(act, sy_done[q], i, 2)
                        for s in range(SH):
                            act.wait_ge(shid_done[q], SH * i + s + 1)
                            act.activation(h_hi[q][:, s], s_hid[q][:, s, :], ACT.Copy).then_inc(sh_hi_done[q], 1)

                run_three_stages(act, step, NG // 2)

            @block.vector
            def _(dve):
                dve.wait_ge(sw_hi_done, 2)
                dve.tensor_tensor(sw13_lo[:].rearrange("p w c s h -> p (w c s h)"), work_b[0][:, 0:1024],
                                  sw13_hi[:].rearrange("p w c s h -> p (w c s h)").bitcast(F32),
                                  ALU.subtract).then_inc(sw_lo_done, 1)
                dve.tensor_tensor(sw2_lo[:], sw2_raw, sw2_hi[:].bitcast(F32), ALU.subtract).then_inc(sw_lo_done, 1)
                dve.wait_ge(sw_lo_done, 2)

                def step(a, bb, c):
                    if bb:
                        i, q = bb
                        wait_reuse(dve, sh_lo_done[q], i, SH)
                        wait_reuse(dve, sh_hi_done[q], i, SH)
                        for s in range(SH):
                            dve.wait_ge(ssilu_done[q], SH * i + s + 1)
                            dve.wait_ge(su_done[q], SH * i + s + 1)
                            dve.tensor_tensor(s_hid[q][:, s, :], s_silu[q][:, s, :], psS[s][1][:], ALU.mult)\
                                .then_inc(shid_done[q], 1)
                    if a:
                        i, q = a
                        wait_reuse(dve, su_done[q], i, SH)
                        for ch in range(C):
                            dve.wait_ge(x2T_hi[q], C * i + ch + 1)
                            dve.tensor_tensor(xT_lo[q][:, ch], psT[ch][:], xT_hi[q][:, ch].bitcast(F32),
                                              ALU.subtract).then_inc(x2T_lo[q], 1)
                    if bb:
                        i, q = bb
                        wait_reuse(dve, sy_done[q], i, 2)
                        for s in range(SH):
                            dve.wait_ge(sh_hi_done[q], SH * i + s + 1)
                            dve.tensor_tensor(h_lo[q][:, s], s_hid[q][:, s, :], h_hi[q][:, s].bitcast(F32),
                                              ALU.subtract).then_inc(sh_lo_done[q], 1)
                    if c:
                        i, q = c
                        dve.wait_ge(res_loaded[q], 16 * (i + 1))
                        dve.wait_ge(now_set[q], 2 * (i + 1))
                        for t in range(G):
                            dve.wait_ge(sy_done[q], 2 * i + t // 2 + 1)
                            dve.scalar_tensor_tensor(res[q][:, t, :], psY[t // 2][:, t % 2 * N:(t % 2 + 1) * N],
                                                     tok_now[q][:, 2, t:t + 1], res[q][:, t, :], ALU.add,
                                                     ALU.add).then_inc(base_done[q], 1)
                        dve.wait_ge(pair_gathered[q], 16 * K2 * (i + 1))
                        for k, (ready, done) in enumerate(((base_done, one_done), (one_done, res_done))):
                            for t in range(G):
                                dve.wait_ge(ready[q], G * i + t + 1)
                                dve.scalar_tensor_tensor(res[q][:, t, :], pair_rows[q][:, TOPK * t + k, :],
                                                         tok_now[q][:, 3 + k, t:t + 1], res[q][:, t, :], ALU.mult,
                                                         ALU.add).then_inc(done[q], 1)

                run_three_stages(dve, step, NG // 2)

            @block.tensor
            def _(pe):
                pe.wait_ge(sw_hi_done, 2)
                pe.wait_ge(sw_lo_done, 2)

                def step(a, bb, c):
                    if a:
                        i, q = a
                        pe.wait_ge(ln2_done[q], G * (i + 1))
                        wait_before(pe, x2T_hi, a, C)
                        wait_before(pe, x2T_lo, a, C)
                        for ch in range(C):
                            for t in range(G):
                                last = pe.transpose(psT[ch][:, t * P:(t + 1) * P], xn[q][:, t, ch::C], ident[:])
                            last.then_inc(x2T_done[q], 1)
                    if bb:
                        i, q = bb
                        pe.wait_ge(x2T_hi[q], C * (i + 1))
                        pe.wait_ge(x2T_lo[q], C * (i + 1))
                        wait_before(pe, ssilu_done, bb, SH)
                        wait_before(pe, shid_done, bb, SH)
                        for s in range(SH):
                            for k, done in enumerate((sg_done, su_done)):
                                three_passes(pe, psS[s][k][:], [
                                    ((sw13_hi[:, k, ch, s], sw13_lo[:, k, ch, s]),
                                     (xT_hi[q][:, ch], xT_lo[q][:, ch])) for ch in range(C)]).then_inc(done[q], 1)
                    if c:
                        i, q = c
                        pe.wait_ge(sh_hi_done[q], SH * (i + 1))
                        pe.wait_ge(sh_lo_done[q], SH * (i + 1))
                        wait_before(pe, base_done, c, G)
                        for j in range(2):
                            for t in (2 * j, 2 * j + 1):
                                last = three_passes(pe, psY[j][:, t % 2 * N:(t % 2 + 1) * N], [
                                    ((h_hi[q][:, s, t * P:(t + 1) * P], h_lo[q][:, s, t * P:(t + 1) * P]),
                                     (sw2_hi[:, s], sw2_lo[:, s])) for s in range(SH)])
                            last.then_inc(sy_done[q], 1)

                run_three_stages(pe, step, NG // 2)


_INS = ['x', 'adj', 'L0_gnn_b', 'L0_ffn_gate_w', 'L0_ffn_w1', 'L0_ffn_w3', 'L0_ffn_w2', 'L0_ffn_sw1', 'L0_ffn_sw3',
        'L0_ffn_sw2']
_OUTS = [((128, 128, 256), 'float32')]


def kernel(**inputs):
    import numpy as _np
    import concourse.bacc as _bacc
    from concourse import mybir as _mybir
    from concourse.bass_utils import run_bass_kernel_spmd as _run

    nc = _bacc.Bacc("TRN2", target_bir_lowering=False, num_devices=1)
    arrays, args = {}, []
    for name in _INS:
        a = _np.ascontiguousarray(inputs[name])
        arrays[f"in_{name}_dram"] = a
        args.append(nc.dram_tensor(f"in_{name}_dram", a.shape, _mybir.dt.from_np(a.dtype), kind="ExternalInput").ap())
    for i, (shape, dtype) in enumerate(_OUTS):
        dt = _mybir.dt.from_np(_np.dtype(dtype))
        args.append(nc.dram_tensor(f"out_{i}_dram", shape, dt, kind="ExternalOutput").ap())
    build(nc, *args)
    r = _run(nc, [arrays], core_ids=[0])
    return r.results[0]["out_0_dram"]
```

```python
import concourse.bass as bass
from concourse import mybir
from contextlib import ExitStack


F32 = mybir.dt.float32
F32R = mybir.dt.float32r
BF16 = mybir.dt.bfloat16
FP16 = mybir.dt.float16
U32 = mybir.dt.uint32
ACT = mybir.ActivationFunctionType
ALU = mybir.AluOpType
AX = mybir.AxisListType

P = 128
CAP = 512
TOPK = 2
ROUTE_SCALE = 2.5
EPS = 1e-5
G = 4
REC = 7 * G


def run_stages(engine, step, depth, pairs, peeled=1):
    def items(j, r, known):
        at = []
        for d in range(depth):
            q = (r - d) % 2
            i = j + (r - d - q) // 2
            at.append((i, q) if not known or 0 <= i < pairs else None)
        return at

    first = (depth + 2) // 2
    for n in range(2 * first):
        step(*items(0, n, True))
    with engine.Fori(first, pairs - peeled) as j:
        for r in range(2):
            step(*items(j, r, False))
    for n in range(2 * (pairs - peeled), 2 * pairs + depth - 1):
        step(*items(0, n, True))


def run_pairs(engine, step, pairs):
    for q in range(2):
        step(0, q)
    with engine.Fori(1, pairs) as i:
        for q in range(2):
            step(i, q)


def wait_before(engine, sems, at, n):
    i, q = at
    if q == 1:
        engine.wait_ge(sems[0], (i + 1) * n)
    elif not (isinstance(i, int) and i == 0):
        engine.wait_ge(sems[1], i * n)


def wait_reuse(engine, sem, i, n):
    if not (isinstance(i, int) and i == 0):
        engine.wait_ge(sem, i * n)


def pass_waits(engine, passed):
    engine.sem_inc(passed, 1)


def build(nc, x, adj, b, gate_w, w1, w3, w2, sw1, sw3, sw2, out):
    B, D, N = x.shape
    E, _, H = w1.shape
    SH = sw1.shape[1] // P
    C = N // P
    S = CAP // P
    NG = B // G
    K2 = G * TOPK
    assert D == P and H == P and S == G and C == 2 and SH == 2 and 2 * E == P

    xn_dram = nc.dram_tensor("xn_rows", [B * D, N], F32, kind="Internal").ap()
    xnT_dram = nc.dram_tensor("xn_columns", [NG, P, C * 512], F32, kind="Internal").ap()
    y_dram = nc.dram_tensor("slot_rows", [E * CAP, N], F32, kind="Internal").ap()

    ctx = ExitStack()
    with ctx:
        def sb(name, shape, dt):
            return ctx.enter_context(nc.sbuf_tensor(name, shape, dt))

        def sb2(name, shape, dt):
            return [sb(f"{name}{q}", shape, dt) for q in range(2)]

        def sem(name):
            return ctx.enter_context(nc.semaphore(name))

        def sem2(name):
            return [sem(f"{name}{q}") for q in range(2)]

        passed = {engine: sem(f"passed_{engine}") for engine in ("pool", "dve", "pe")}

        bank = [ctx.enter_context(nc.psum_tensor(f"bank{k}", [P, 512], F32)) for k in range(8)]

        ident = sb("ident", [P, P], F32)
        ones = sb("ones", [P, P], BF16)
        before = sb("before", [P, P], BF16)
        zero = sb("zero", [P, 512], BF16)
        slot_iota = sb("slot_iota", [P, CAP], FP16)
        expert_iota = sb("expert_iota", [P, E], F32)
        part_iota = sb("part_iota", [P, 1], F32)
        tile_iota = sb("tile_iota", [P, B], F32)
        minus_half = sb("minus_half", [P, G], F32)
        minus_one = sb("minus_one", [P, G], F32)
        eps = sb("eps", [P, G], F32)
        join = sb("join", [P, E], F32)
        adj_raw = sb("adj_raw", [P, P], F32)
        adjT = sb("adjT", [P, P], F32)
        gate_raw = sb("gate_raw", [E, N], F32)
        gateT = sb("gateT", [P, C, E], F32)
        bias = sb("bias", [P, 1], F32)
        rec_all = sb("rec_all", [P, NG, REC], F32)
        tok_all = sb("tok_all", [P, NG, 5, G], F32)
        slot_all = sb("slot_all", [P, NG, K2], U32)
        token_of = sb("token_of", [P, E, S], U32)

        x_in = sb2("x_in", [P, G, N], F32)
        xn = sb2("xn", [P, G, N], F32)
        xT_hi = sb2("xT_hi", [P, C, 512], F32R)
        xT_lo = sb2("xT_lo", [P, C, 512], F32R)
        work_a = sb2("work_a", [P, 4096], F32)
        work_b = sb2("work_b", [P, 2048], F32)

        res = sb2("res", [P, G, N], F32)
        sw13_hi = sb("sw13_hi", [P, 2, C, SH, P], F32R)
        sw13_lo = sb("sw13_lo", [P, 2, C, SH, P], F32R)
        sw2_hi = sb("sw2_hi", [P, SH, N], F32R)
        sw2_lo = sb("sw2_lo", [P, SH, N], F32R)
        sw13_raw = res[0][:].rearrange("p t n -> p (t n)").rearrange("p (w n) -> p w n", w=2)
        sw2_raw = res[1][:, 0:SH, :]
        sw_loaded = sem("sw_loaded")
        sw_hi_done = sem("sw_hi_done")
        sw_lo_done = sem("sw_lo_done")

        stats = sb2("stats", [P, G, 6], F32)
        mv = sb2("mv", [P, G, 2], F32)
        var_eps = sb2("var_eps", [P, G], F32)
        norm = sb2("norm", [P, 2, G], F32)
        neg_rstd = sb2("neg_rstd", [P, G], F32)
        xT = [work_b[q][:, 0:C * 512].rearrange("p (c t) -> p c t", c=C) for q in range(2)]
        logitT = [work_b[q][0:E, C * 512:C * 512 + 512] for q in range(2)]
        score = [work_b[q][:, 1536:1536 + G * E].rearrange("p (t e) -> p t e", t=G) for q in range(2)]
        top8 = sb2("top8", [P, G, 8], F32)
        idx8 = sb2("idx8", [P, G, 8], U32)
        rec = sb2("rec", [P, REC], F32)
        onehot = sb2("onehot", [P, G, TOPK, E], BF16)
        mask = sb2("mask", [P, G, E], BF16)
        seen = sb2("seen", [P, G, E], BF16)
        tagged = sb2("tagged", [P, K2, 2, E], BF16)
        posdot = sb("posdot", [P, K2, E], F32)
        at_pos = [work_a[q][:, 0:2048].bitcast(BF16).rearrange("p (k s) -> p k s", k=K2) for q in range(2)]

        s_const = sem("s_const")
        s_raw = [sem(f"s_raw{k}") for k in range(3)]
        s_wT = sem("s_wT")
        s_wTc = sem("s_wTc")
        x_loaded = sem2("x_loaded")
        stats_done = sem2("stats_done")
        mv_done = sem2("mv_done")
        norm_step = sem2("norm_step")
        norm_saved = sem2("norm_saved")
        ln_done = sem2("ln_done")
        xn_stored = sem2("xn_stored")
        xnT_done = sem2("xnT_done")
        xT_done = sem2("xT_done")
        xT_stored = sem2("xT_stored")
        gate_done = sem2("gate_done")
        logitT_done = sem2("logitT_done")
        logit_done = sem2("logit_done")
        score_done = sem2("score_done")
        gnn_done = sem2("gnn_done")
        gmax_done = sem2("gmax_done")
        top_done = sem2("top_done")
        idx_done = sem2("idx_done")
        pick_done = sem2("pick_done")
        onehot_done = sem2("onehot_done")
        mask_done = sem2("mask_done")
        seen_done = sem2("seen_done")
        tagged_done = sem2("tagged_done")
        prefix_done = sem2("prefix_done")
        posdot_done = sem2("posdot_done")
        pos_done = sem2("pos_done")
        at_done = sem2("at_done")
        table_done = sem2("table_done")
        rec_saved = sem2("rec_saved")
        s_table = sem("s_table")
        s_tabc = sem("s_tabc")
        s_join = sem("s_join")
        s_fin = sem("s_fin")

        psT, psG, psA, psL, psP, psTab = bank[0:2], bank[2], bank[3:5], bank[5], bank[6], bank[7]

        with nc.Block() as block:
            @block.sync
            def _(sp):
                def load(i, q):
                    tile0 = (2 * i + q) * G
                    sp.dma_start(x_in[q][:], x[bass.ds(tile0, G)].rearrange("t d n -> d t n"))\
                        .then_inc(x_loaded[q], 16)

                def store(i, q):
                    sp.wait_ge(ln_done[q], G * (i + 1))
                    row0 = (2 * i + q) * G * D
                    sp.dma_start(xn_dram[bass.ds(row0, G * D)].rearrange("(t d) n -> d t n", t=G), xn[q][:])\
                        .then_inc(xn_stored[q], 16)

                def store_T(i, q):
                    sp.wait_ge(xT_done[q], C * (i + 1))
                    sp.dma_start(xnT_dram[2 * i + q], xT[q].rearrange("p c t -> p (c t)"))\
                        .then_inc(xT_stored[q], 16)

                def step(z, a):
                    if z:
                        i, q = z
                        store(i, q)
                        if not isinstance(i, int) or i + 1 < NG // 2:
                            load(i + 1, q)
                    if a:
                        store_T(*a)

                load(0, 0)
                load(0, 1)
                sp.dma_start(adj_raw[:], adj).then_inc(s_raw[0], 16)
                sp.dma_start(gate_raw[:], gate_w).then_inc(s_raw[1], 16)
                sp.dma_start(bias[:], b.rearrange("(d a) -> d a", a=1)).then_inc(s_raw[2], 16)
                for k, w in enumerate((sw1, sw3)):
                    sp.dma_start(sw13_raw[:, k],
                                 w.rearrange("(p c) h -> p (c h)", c=C)).then_inc(sw_loaded, 16)
                sp.dma_start(sw2_raw, sw2.rearrange("(s p) n -> p s n", s=SH)).then_inc(sw_loaded, 16)
                run_stages(sp, step, 2, NG // 2)
                for q in range(2):
                    sp.wait_ge(xn_stored[q], 16 * (NG // 2))
                    sp.wait_ge(xT_stored[q], 16 * (NG // 2))

            @block.gpsimd
            def _(pool):
                pool.memset(ident[:], 0.0).then_inc(s_const, 1)
                pool.memset(before[:], 1.0).then_inc(s_const, 1)
                pool.memset(join[:], 0.0).then_inc(s_const, 1)
                pool.memset(ones[:], 1.0).then_inc(s_const, 1)
                pool.memset(zero[:], 0.0).then_inc(s_const, 1)
                pool.memset(minus_half[:], -0.5).then_inc(s_const, 1)
                pool.memset(minus_one[:], -1.0).then_inc(s_const, 1)
                pool.memset(eps[:], EPS).then_inc(s_const, 1)
                pool.memset(seen[0][:, 0, :], 0.0).then_inc(s_const, 1)
                pool.iota(slot_iota[:], [[1, CAP]], base=0, channel_multiplier=0,
                          allow_small_or_imprecise_dtypes=True).then_inc(s_const, 1)
                pool.iota(expert_iota[:], [[1, E]], base=0, channel_multiplier=0,
                          allow_small_or_imprecise_dtypes=True).then_inc(s_const, 1)
                pool.iota(part_iota[:], [[0, 1]], base=0, channel_multiplier=1,
                          allow_small_or_imprecise_dtypes=True).then_inc(s_const, 1)
                pool.iota(tile_iota[:], [[1, B]], base=0, channel_multiplier=0,
                          allow_small_or_imprecise_dtypes=True).then_inc(s_const, 1)
                pool.wait_ge(s_const, 13)
                pool.affine_select(out=ident[:], in_=ident[:], compare_op=ALU.not_equal, fill=1.0, base=0,
                                   pattern=[[-1, P]], channel_multiplier=1).then_inc(s_const, 1)
                pool.affine_select(out=before[:], in_=before[:], compare_op=ALU.is_gt, fill=0.0, base=0,
                                   pattern=[[1, P]], channel_multiplier=-1).then_inc(s_const, 1)
                pool.affine_select(out=join[:], in_=join[:], compare_op=ALU.not_equal, fill=1.0, base=0,
                                   pattern=[[-1, E]], channel_multiplier=1).then_inc(s_const, 1)
                pool.wait_ge(s_const, 16)
                pool.affine_select(out=join[:], in_=join[:], compare_op=ALU.not_equal, fill=float(P), base=-E,
                                   pattern=[[-1, E]], channel_multiplier=1).then_inc(s_const, 1)

                def step(z, a, bb, c):
                    if z:
                        i, q = z
                        pool.wait_ge(mv_done[q], G * (i + 1))
                        wait_reuse(pool, ln_done[q], i, G)
                        pool.tensor_tensor(var_eps[q][:], mv[q][:, :, 1], eps[:], ALU.add)\
                            .then_inc(norm_step[q], 1)
                        pool.wait_ge(norm_step[q], 4 * i + 1)
                        pool.tensor_tensor(norm[q][:, 0, :], var_eps[q][:], minus_half[:], ALU.pow)\
                            .then_inc(norm_step[q], 1)
                        pool.wait_ge(norm_step[q], 4 * i + 2)
                        pool.tensor_tensor(neg_rstd[q][:], norm[q][:, 0, :], minus_one[:], ALU.mult)\
                            .then_inc(norm_step[q], 1)
                        pool.wait_ge(norm_step[q], 4 * i + 3)
                        pool.tensor_tensor(norm[q][:, 1, :], neg_rstd[q][:], mv[q][:, :, 0], ALU.mult)\
                            .then_inc(norm_step[q], 1)
                        pool.wait_ge(norm_step[q], 4 * i + 4)
                        pool.tensor_copy(tok_all[:, 2 * i + q, 0:2, :], norm[q][:]).then_inc(norm_saved[q], 1)
                    if bb:
                        i, q = bb
                        oh = onehot[q][:].rearrange("p t k e -> p (t k) e")
                        pool.wait_ge(onehot_done[q], i + 1)
                        wait_reuse(pool, prefix_done[q], i, 1)
                        pool.tensor_tensor(mask[q][:], onehot[q][:, :, 0, :], onehot[q][:, :, 1, :], ALU.add)\
                            .then_inc(mask_done[q], 1)
                        pool.wait_ge(mask_done[q], i + 1)
                        for t in range(1, G):
                            pool.tensor_tensor(seen[q][:, t, :], seen[q][:, t - 1, :], mask[q][:, t - 1, :],
                                               ALU.add).then_inc(seen_done[q], 1)
                            pool.wait_ge(seen_done[q], G * i + t)
                        wait_before(pool, prefix_done, bb, 1)
                        pool.tensor_tensor(seen[1 - q][:, 0, :], seen[q][:, G - 1, :], mask[q][:, G - 1, :],
                                           ALU.add).then_inc(seen_done[q], 1)
                        wait_reuse(pool, table_done[q], i, 1)
                        pass_waits(pool, passed["pool"])
                        pool.tensor_scalar(tagged[q][:, :, 0, :], oh, part_iota[:, 0:1], 1.0, ALU.mult, ALU.mult)\
                            .then_inc(tagged_done[q], 1)
                        group = 2 * i + q
                        pool.tensor_tensor(
                            tagged[q][:, :, 1, :].rearrange("p (t k) e -> p t k e", k=TOPK), onehot[q][:],
                            tile_iota[:, bass.ds(group * G, G)].unsqueeze(2).unsqueeze(3)
                            .to_broadcast([P, G, TOPK, E]), ALU.mult).then_inc(tagged_done[q], 1)
                        pool.wait_ge(seen_done[q], G * (i + 1))
                    if c:
                        i, q = c
                        pool.wait_ge(pos_done[q], i + 1)
                        pool.wait_ge(gmax_done[q], G // 2 * (i + 1))
                        pool.tensor_copy(rec_all[:, 2 * i + q, :], rec[q][:]).then_inc(rec_saved[q], 1)

                run_stages(pool, step, 4, NG // 2)

            @block.scalar
            def _(act):
                def step(z, a, bb, c):
                    if a:
                        i, q = a
                        wait_reuse(act, xT_stored[q], i, 16)
                        wait_reuse(act, gate_done[q], i, 1)
                        for ch in range(C):
                            act.wait_ge(xnT_done[q], C * i + ch + 1)
                            act.activation(xT[q][:, ch, :], psT[ch][:], ACT.Copy).then_inc(xT_done[q], 1)
                        act.wait_ge(gate_done[q], i + 1)
                        wait_reuse(act, logit_done[q], i, 1)
                        act.activation(logitT[q], psG[0:E, :], ACT.Copy).then_inc(logitT_done[q], 1)
                    if z:
                        i, q = z
                        act.wait_ge(norm_step[q], 4 * (i + 1))
                        act.wait_ge(x_loaded[q], 16 * (i + 1))
                        wait_reuse(act, xn_stored[q], i, 16)
                        wait_reuse(act, gnn_done[q], i, G // 2)
                        for t in range(G):
                            act.activation(xn[q][:, t, :], x_in[q][:, t, :], ACT.Identity,
                                           bias=norm[q][:, 1, t:t + 1], scale=norm[q][:, 0, t:t + 1])\
                                .then_inc(ln_done[q], 1)
                    if a:
                        i, q = a
                        act.wait_ge(logit_done[q], i + 1)
                        wait_reuse(act, idx_done[q], i, G)
                        act.activation(score[q], psL[:, 0:G * E].rearrange("p (t e) -> p t e", t=G),
                                       ACT.Sigmoid).then_inc(score_done[q], 1)

                run_stages(act, step, 4, NG // 2)
                act.wait_ge(sw_loaded, 48)
                act.activation(sw13_hi[:].rearrange("p w c s h -> p w (c s h)"), sw13_raw, ACT.Copy)\
                    .then_inc(sw_hi_done, 1)
                act.activation(sw2_hi[:], sw2_raw, ACT.Copy).then_inc(sw_hi_done, 1)
                act.wait_ge(s_table, 1)
                wait_before(act, at_done, (NG // 2, 0), K2)
                act.activation(work_a[0][:, 0:512], psTab[:], ACT.Copy).then_inc(s_tabc, 1)

            @block.vector
            def _(dve):
                dve.wait_ge(s_wT, 2)
                dve.tensor_copy(adjT[:], psA[0][:, 0:P]).then_inc(s_wTc, 1)
                dve.tensor_copy(gateT[:].rearrange("p c e -> p (c e)"), psA[1][:, 0:C * E]).then_inc(s_wTc, 1)

                def step(z, a, bb, c):
                    if z:
                        i, q = z
                        dve.wait_ge(x_loaded[q], 16 * (i + 1))
                        for t in range(G):
                            dve.bn_stats(stats[q][:, t, :], x_in[q][:, t, :]).then_inc(stats_done[q], 1)
                    if bb:
                        i, q = bb
                        wait_reuse(dve, rec_saved[q], i, 1)
                        for j in range(G // 2):
                            dve.wait_ge(gnn_done[q], G // 2 * i + j + 1)
                            dve.reduce_max(rec[q][:, 3 * K2 + 2 * j:3 * K2 + 2 * j + 2],
                                           psA[j][:].rearrange("p (t n) -> p t n", t=2), AX.X)\
                                .then_inc(gmax_done[q], 1)
                    if z:
                        i, q = z
                        wait_reuse(dve, norm_step[q], i, 4)
                        dve.wait_ge(stats_done[q], G * (i + 1))
                        pass_waits(dve, passed["dve"])
                        for t in range(G):
                            dve.bn_aggr(mv[q][:, t, :], stats[q][:, t, :]).then_inc(mv_done[q], 1)
                    if bb:
                        i, q = bb
                        dve.wait_ge(score_done[q], i + 1)
                        wait_reuse(dve, pick_done[q], i, 2)
                        pass_waits(dve, passed["dve"])
                        for t in range(G):
                            dve.max(top8[q][:, t, :], score[q][:, t, :]).then_inc(top_done[q], 1)
                    if c:
                        i, q = c
                        dve.wait_ge(prefix_done[q], i + 1)
                        dve.wait_ge(onehot_done[q], i + 1)
                        wait_before(dve, pos_done, c, 1)
                        dve.tensor_tensor(
                            posdot[:].rearrange("p (t k) e -> p t k e", k=TOPK), onehot[q][:],
                            psP[:, 0:G * E].rearrange("p (t e) -> p t e", t=G).unsqueeze(2)
                            .to_broadcast([P, G, TOPK, E]), ALU.mult).then_inc(posdot_done[q], 1)
                    if bb:
                        i, q = bb
                        dve.wait_ge(top_done[q], G * (i + 1))
                        dve.tensor_copy(rec[q][:, 0:K2].rearrange("p (t k) -> p t k", k=TOPK),
                                        top8[q][:, :, 0:TOPK]).then_inc(pick_done[q], 1)
                        for t in range(G):
                            dve.max_index(idx8[q][:, t, :], top8[q][:, t, :], score[q][:, t, :])\
                                .then_inc(idx_done[q], 1)
                    if c:
                        i, q = c
                        dve.wait_ge(posdot_done[q], i + 1)
                        dve.reduce_sum(rec[q][:, 2 * K2:3 * K2], posdot[:], AX.X).then_inc(pos_done[q], 1)
                    if bb:
                        i, q = bb
                        dve.wait_ge(idx_done[q], G * (i + 1))
                        dve.tensor_copy(rec[q][:, K2:2 * K2].rearrange("p (t k) -> p t k", k=TOPK),
                                        idx8[q][:, :, 0:TOPK]).then_inc(pick_done[q], 1)

                    def place(ks):
                        i, q = c
                        for k in ks:
                            dve.tensor_scalar(at_pos[q][:, k, :], slot_iota[:],
                                              rec[q][:, 2 * K2 + k:2 * K2 + k + 1], None, ALU.is_equal)\
                                .then_inc(at_done[q], 1)

                    if c:
                        i, q = c
                        dve.wait_ge(pos_done[q], i + 1)
                        wait_reuse(dve, table_done[q], i, 1)
                        place([0])
                    if bb:
                        i, q = bb
                        dve.wait_ge(pick_done[q], 2 * (i + 1))
                        wait_reuse(dve, tagged_done[q], i, 2)
                        dve.tensor_tensor(onehot[q][:].rearrange("p t k e -> p (t k) e"),
                                          rec[q][:, K2:2 * K2].unsqueeze(2).to_broadcast([P, K2, E]),
                                          expert_iota[:].unsqueeze(1).to_broadcast([P, K2, E]),
                                          ALU.is_equal).then_inc(onehot_done[q], 1)
                    if c:
                        place(range(1, K2))

                dve.wait_ge(s_const, 17)
                run_stages(dve, step, 4, NG // 2)

                for q in range(2):
                    dve.wait_ge(rec_saved[q], NG // 2)
                    dve.wait_ge(norm_saved[q], NG // 2)
                dve.wait_ge(s_raw[2], 16)
                fin = [0]

                def after(ins):
                    fin[0] += 1
                    ins.then_inc(s_fin, 1)
                    dve.wait_ge(s_fin, fin[0])

                for q in range(2):
                    dve.wait_ge(table_done[q], NG // 2)
                fa = work_a[1]
                total = fa[:, 0:B].rearrange("p (g t) -> p g t", t=G)
                kept = fa[:, B:3 * B].rearrange("p (g k) -> p g k", k=K2)
                scaled = fa[:, 3 * B:5 * B].rearrange("p (g k) -> p g k", k=K2)
                clipped = fa[:, 5 * B:7 * B].rearrange("p (g k) -> p g k", k=K2)
                rmax = fa[:, 7 * B:8 * B].rearrange("p (g t) -> p g t", t=G)
                s_of = rec_all[:, :, 0:K2].rearrange("p g (t k) -> p g t k", k=TOPK)
                pos_of = rec_all[:, :, 2 * K2:3 * K2]
                after(dve.tensor_tensor(total, s_of[:, :, :, 0], s_of[:, :, :, 1], ALU.add))
                after(dve.tensor_scalar(total, total, 1e-20, None, ALU.add))
                after(dve.reciprocal(total, total))
                after(dve.tensor_scalar(kept, pos_of, float(CAP), ROUTE_SCALE, ALU.is_lt, ALU.mult))
                after(dve.tensor_tensor(scaled, kept, rec_all[:, :, 0:K2], ALU.mult))
                sc4 = scaled.rearrange("p g (t k) -> p g t k", k=TOPK)
                for k in range(TOPK):
                    after(dve.tensor_tensor(tok_all[:, :, 3 + k, :], sc4[:, :, :, k], total, ALU.mult))
                after(dve.tensor_scalar(clipped, pos_of, float(CAP - 1), None, ALU.min))
                after(dve.scalar_tensor_tensor(slot_all[:], rec_all[:, :, K2:2 * K2], float(CAP), clipped,
                                               ALU.mult, ALU.add))
                after(dve.tensor_scalar(tok_all[:, :, 2, :], rec_all[:, :, 3 * K2:3 * K2 + G], bias[:, 0:1], 0.0,
                                        ALU.add, ALU.max))
                dve.wait_ge(sw_hi_done, 2)
                dve.tensor_tensor(sw13_lo[:].rearrange("p w c s h -> p w (c s h)"), sw13_raw,
                                  sw13_hi[:].rearrange("p w c s h -> p w (c s h)").bitcast(F32),
                                  ALU.subtract).then_inc(sw_lo_done, 1)
                dve.tensor_tensor(sw2_lo[:], sw2_raw, sw2_hi[:].bitcast(F32), ALU.subtract).then_inc(sw_lo_done, 1)
                dve.wait_ge(s_join, 1)
                dve.tensor_copy(token_of[:].rearrange("p e s -> p s e"),
                                psA[0][:, 0:S * E].rearrange("p (s e) -> p s e", s=S))

            @block.tensor
            def _(pe):
                pe.wait_ge(s_const, 17)
                pe.wait_ge(s_raw[0], 16)
                pe.transpose(psA[0][:, 0:P], adj_raw[:], ident[:]).then_inc(s_wT, 1)
                pe.wait_ge(s_raw[1], 16)
                for ch in range(C):
                    last = pe.transpose(psA[1][:, ch * E:(ch + 1) * E], gate_raw[:, ch::C], ident[0:E, 0:E])
                last.then_inc(s_wT, 1)
                pe.matmul(psTab[:], zero[:, 0:P], zero[:], start=True, stop=False)
                pe.wait_ge(s_wTc, 2)

                def step(z, a, bb, c):
                    if a:
                        i, q = a
                        pe.wait_ge(ln_done[q], G * (i + 1))
                        wait_before(pe, xT_done, a, C)
                        for ch in range(C):
                            for t in range(G):
                                last = pe.transpose(psT[ch][:, t * P:(t + 1) * P], xn[q][:, t, ch::C], ident[:])
                            last.then_inc(xnT_done[q], 1)
                        wait_before(pe, gmax_done, a, G // 2)

                        def neighbours(j):
                            pe.matmul(psA[j][:], adjT[:],
                                      xn[q][:, 2 * j:2 * j + 2, :].rearrange("p t n -> p (t n)"),
                                      start=True, stop=True).then_inc(gnn_done[q], 1)

                        neighbours(0)
                        pe.wait_ge(xT_done[q], C * (i + 1))
                        wait_before(pe, logitT_done, a, 1)
                        for ch in range(C):
                            last = pe.matmul(psG[0:E, :], gateT[:, ch, :], xT[q][:, ch, :],
                                             start=(ch == 0), stop=(ch == C - 1))
                        last.then_inc(gate_done[q], 1)
                        neighbours(1)
                        pe.wait_ge(logitT_done[q], i + 1)
                        wait_before(pe, score_done, a, 1)
                        pass_waits(pe, passed["pe"])
                        for t in range(G):
                            last = pe.transpose(psL[:, t * E:(t + 1) * E], logitT[q][:, t * P:(t + 1) * P],
                                                ident[0:E, 0:E])
                        last.then_inc(logit_done[q], 1)
                    if bb:
                        i, q = bb
                        pe.wait_ge(seen_done[q], G * i + G - 1)
                        wait_before(pe, seen_done, bb, G)
                        wait_before(pe, posdot_done, bb, 1)
                        pe.matmul(psP[:, 0:G * E], before[:], mask[q][:].rearrange("p t e -> p (t e)"),
                                  start=True, stop=False)
                        pe.matmul(psP[:, 0:G * E], ones[:], seen[q][:].rearrange("p t e -> p (t e)"),
                                  start=False, stop=True).then_inc(prefix_done[q], 1)
                    if c:
                        i, q = c
                        pe.wait_ge(at_done[q], K2 * (i + 1))
                        pe.wait_ge(tagged_done[q], 2 * (i + 1))
                        for k in range(K2):
                            last = pe.matmul(psTab[:], tagged[q][:, k].rearrange("p a e -> p (a e)"),
                                             at_pos[q][:, k, :], start=False, stop=False)
                        last.then_inc(table_done[q], 1)

                run_stages(pe, step, 4, NG // 2)
                pe.matmul(psTab[:], zero[:, 0:P], zero[:], start=False, stop=True).then_inc(s_table, 1)
                pe.wait_ge(s_tabc, 1)
                for q in range(2):
                    pe.wait_ge(gmax_done[q], G // 2 * (NG // 2))
                for s in range(S):
                    last = pe.matmul(psA[0][:, s * E:(s + 1) * E], work_a[0][:, s:512:S], join[:],
                                     start=True, stop=True)
                last.then_inc(s_join, 1)

        w13_raw = [work_a[q][:, 0:512].rearrange("p (w c h) -> p w c h", w=2, c=C) for q in range(2)]
        w2_raw = [work_a[q][:, 512:768] for q in range(2)]
        w13_hi = sb2("w13_hi", [P, 2, C, H], F32R)
        w13_lo = sb2("w13_lo", [P, 2, C, H], F32R)
        w2_hi = sb2("w2_hi", [P, N], F32R)
        w2_lo = sb2("w2_lo", [P, N], F32R)
        rows = xn
        token_now = sb2("token_now", [P, S], U32)
        silu = [work_b[q][:, 0:512] for q in range(2)]
        hid = [work_b[q][:, 512:1024] for q in range(2)]
        h_hi = sb2("h_hi", [P, SH, 512], F32R)
        h_lo = sb2("h_lo", [P, SH, 512], F32R)
        y_out = x_in

        w13_loaded = sem2("w13_loaded")
        w2_loaded = sem2("w2_loaded")
        w13_hi_done = sem2("w13_hi_done")
        w13_lo_done = sem2("w13_lo_done")
        w2_hi_done = sem2("w2_hi_done")
        w2_lo_done = sem2("w2_lo_done")
        token_set = sem2("token_set")
        gathered = sem2("gathered")
        rowsT_done = sem2("rowsT_done")
        rT_hi_done = sem2("rT_hi_done")
        rT_lo_done = sem2("rT_lo_done")
        g_done = sem2("g_done")
        u_done = sem2("u_done")
        silu_done = sem2("silu_done")
        hid_done = sem2("hid_done")
        h_hi_done = sem2("h_hi_done")
        h_lo_done = sem2("h_lo_done")
        y_done = sem2("y_done")
        y_act = sem2("y_act")
        y_dve = sem2("y_dve")
        y_stored = sem2("y_stored")

        def three_passes(pe, ps, terms):
            products = [(wv, mv_) for (w_hi, w_lo), (m_hi, m_lo) in terms
                        for wv, mv_ in ((w_hi, m_hi), (w_hi, m_lo), (w_lo, m_hi))]
            for n, (wv, mv_) in enumerate(products):
                last = pe.matmul(ps, wv, mv_, start=(n == 0), stop=(n == len(products) - 1))
            return last

        psT, psGU, psY = bank[0:2], [bank[2:4], bank[4:6]], bank[6:8]

        with nc.Block() as block:
            @block.sync
            def _(sp):
                def load_up(i, q):
                    e = 2 * i + q
                    wait_reuse(sp, w13_lo_done[q], i, 1)
                    wait_reuse(sp, w13_hi_done[q], i, 1)
                    for k, w in enumerate((w1, w3)):
                        sp.dma_start(w13_raw[q][:, k].rearrange("p c h -> p (c h)"),
                                     w[e].rearrange("(p c) h -> p (c h)", c=C)).then_inc(w13_loaded[q], 16)

                def load_down(i, q):
                    e = 2 * i + q
                    wait_reuse(sp, w2_lo_done[q], i, 1)
                    wait_reuse(sp, w2_hi_done[q], i, 1)
                    sp.dma_start(w2_raw[q], w2[e]).then_inc(w2_loaded[q], 16)

                def store(i, q):
                    sp.wait_ge(y_act[q], i + 1)
                    sp.wait_ge(y_dve[q], i + 1)
                    row0 = (2 * i + q) * CAP
                    sp.dma_start(y_dram[bass.ds(row0, CAP)].rearrange("(p s) n -> p (s n)", s=S),
                                 y_out[q][:].rearrange("p s n -> p (s n)")).then_inc(y_stored[q], 16)

                def step(a, bb, c):
                    if a:
                        i, q = a
                        if not isinstance(i, int) or i + 1 < E // 2:
                            load_up(i + 1, q)
                            load_down(i + q, 1 - q)
                        elif q == 0:
                            load_down(i, 1)
                    if c:
                        store(*c)

                load_up(0, 0)
                load_up(0, 1)
                load_down(0, 0)
                run_stages(sp, step, 3, E // 2)
                for q in range(2):
                    sp.wait_ge(y_stored[q], 16 * (E // 2))

            @block.gpsimd
            def _(pool):
                def step(i, q):
                    pool.wait_ge(token_set[q], i + 1)
                    wait_reuse(pool, rowsT_done[q], i, C)
                    pass_waits(pool, passed["pool"])
                    for s in range(S):
                        pool.indirect_dma_start(
                            out=rows[q][:, s, :], out_offset=None, in_=xn_dram,
                            in_offset=bass.IndirectOffsetOnAxis(ap=token_now[q][:, s:s + 1], axis=0))\
                            .then_inc(gathered[q], 16)

                run_pairs(pool, step, E // 2)

            @block.tensor
            def _(pe):
                def step(a, bb, c):
                    if a:
                        i, q = a
                        pe.wait_ge(gathered[q], 16 * S * (i + 1))
                        wait_before(pe, rT_hi_done, a, C)
                        wait_before(pe, rT_lo_done, a, C)
                        for ch in range(C):
                            for s in range(S):
                                last = pe.transpose(psT[ch][:, s * P:(s + 1) * P], rows[q][:, s, ch::C], ident[:])
                            last.then_inc(rowsT_done[q], 1)
                    if bb:
                        i, q = bb
                        pe.wait_ge(w13_hi_done[q], i + 1)
                        pe.wait_ge(w13_lo_done[q], i + 1)
                        pe.wait_ge(rT_hi_done[q], C * (i + 1))
                        pe.wait_ge(rT_lo_done[q], C * (i + 1))
                        wait_reuse(pe, silu_done[q], i, 1)
                        wait_reuse(pe, hid_done[q], i, 1)
                        for k, done in enumerate((g_done, u_done)):
                            three_passes(pe, psGU[q][k][:], [
                                ((w13_hi[q][:, k, ch], w13_lo[q][:, k, ch]), (xT_hi[q][:, ch], xT_lo[q][:, ch]))
                                for ch in range(C)]).then_inc(done[q], 1)
                    if c:
                        i, q = c
                        pe.wait_ge(w2_hi_done[q], i + 1)
                        pe.wait_ge(w2_lo_done[q], i + 1)
                        pe.wait_ge(h_hi_done[q], i + 1)
                        pe.wait_ge(h_lo_done[q], i + 1)
                        wait_before(pe, y_act, c, 1)
                        wait_before(pe, y_dve, c, 1)
                        for j in range(2):
                            for s in (2 * j, 2 * j + 1):
                                last = three_passes(pe, psY[j][:, s % 2 * N:(s % 2 + 1) * N], [
                                    ((h_hi[q][:, 0, s * P:(s + 1) * P], h_lo[q][:, 0, s * P:(s + 1) * P]),
                                     (w2_hi[q][:], w2_lo[q][:]))])
                            last.then_inc(y_done[q], 1)

                run_stages(pe, step, 3, E // 2)

            @block.scalar
            def _(act):
                def set_tokens(i, q):
                    act.activation(token_now[q][:], token_of[:, 2 * i + q, :], ACT.Copy)\
                        .then_inc(token_set[q], 1)

                set_tokens(0, 0)
                set_tokens(0, 1)

                def step(a, bb, c):
                    if a:
                        i, q = a
                        if not isinstance(i, int) or i + 1 < E // 2:
                            act.wait_ge(gathered[q], 16 * S * (i + 1))
                            set_tokens(i + 1, q)
                        wait_reuse(act, u_done[q], i, 1)
                        for ch in range(C):
                            act.wait_ge(rowsT_done[q], C * i + ch + 1)
                            act.activation(xT_hi[q][:, ch], psT[ch][:], ACT.Copy).then_inc(rT_hi_done[q], 1)
                    if bb:
                        i, q = bb
                        act.wait_ge(g_done[q], i + 1)
                        wait_reuse(act, hid_done[q], i, 1)
                        act.activation(silu[q], psGU[q][0][:], ACT.Silu).then_inc(silu_done[q], 1)
                    if a:
                        i, q = a
                        act.wait_ge(w13_loaded[q], 32 * (i + 1))
                        act.activation(w13_hi[q][:], w13_raw[q], ACT.Copy).then_inc(w13_hi_done[q], 1)
                    if bb:
                        i, q = bb
                        act.wait_ge(hid_done[q], i + 1)
                        wait_reuse(act, y_done[q], i, 2)
                        act.activation(h_hi[q][:, 0], hid[q], ACT.Copy).then_inc(h_hi_done[q], 1)
                        act.wait_ge(w2_loaded[q], 16 * (i + 1))
                        act.activation(w2_hi[q][:], w2_raw[q], ACT.Copy).then_inc(w2_hi_done[q], 1)
                    if c:
                        i, q = c
                        act.wait_ge(y_done[q], 2 * i + 1)
                        wait_reuse(act, y_stored[q], i, 16)
                        act.activation(y_out[q][:, 0:2, :].rearrange("p s n -> p (s n)"), psY[0][:], ACT.Copy)\
                            .then_inc(y_act[q], 1)

                run_stages(act, step, 3, E // 2)

            @block.vector
            def _(dve):
                def step(a, bb, c):
                    if a:
                        i, q = a
                        wait_reuse(dve, u_done[q], i, 1)
                        for ch in range(C):
                            dve.wait_ge(rT_hi_done[q], C * i + ch + 1)
                            dve.tensor_tensor(xT_lo[q][:, ch], psT[ch][:], xT_hi[q][:, ch].bitcast(F32),
                                              ALU.subtract).then_inc(rT_lo_done[q], 1)
                    if bb:
                        i, q = bb
                        dve.wait_ge(silu_done[q], i + 1)
                        dve.wait_ge(u_done[q], i + 1)
                        wait_reuse(dve, h_hi_done[q], i, 1)
                        wait_reuse(dve, h_lo_done[q], i, 1)
                        dve.tensor_tensor(hid[q], silu[q], psGU[q][1][:], ALU.mult).then_inc(hid_done[q], 1)
                    if a:
                        i, q = a
                        dve.wait_ge(w13_hi_done[q], i + 1)
                        dve.tensor_tensor(w13_lo[q][:], w13_raw[q], w13_hi[q][:].bitcast(F32), ALU.subtract)\
                            .then_inc(w13_lo_done[q], 1)
                    if bb:
                        i, q = bb
                        dve.wait_ge(h_hi_done[q], i + 1)
                        wait_reuse(dve, y_done[q], i, 2)
                        dve.tensor_tensor(h_lo[q][:, 0], hid[q], h_hi[q][:, 0].bitcast(F32), ALU.subtract)\
                            .then_inc(h_lo_done[q], 1)
                        dve.wait_ge(w2_hi_done[q], i + 1)
                        dve.tensor_tensor(w2_lo[q][:], w2_raw[q], w2_hi[q][:].bitcast(F32), ALU.subtract)\
                            .then_inc(w2_lo_done[q], 1)
                    if c:
                        i, q = c
                        dve.wait_ge(y_done[q], 2 * (i + 1))
                        wait_reuse(dve, y_stored[q], i, 16)
                        dve.tensor_copy(y_out[q][:, 2:4, :].rearrange("p s n -> p (s n)"), psY[1][:])\
                            .then_inc(y_dve[q], 1)

                run_stages(dve, step, 3, E // 2)

        pair_rows = [work_a[q][:, 0:K2 * N].rearrange("p (k n) -> p k n", k=K2) for q in range(2)]
        x2T = [x_in[q][:].rearrange("p t n -> p (t n)") for q in range(2)]
        slot_now = sb2("slot_now", [P, K2], U32)
        tok_now = sb2("tok_now", [P, 5, G], F32)
        s_silu = [work_b[q][:, 0:1024].rearrange("p (s t) -> p s t", s=SH) for q in range(2)]
        s_hid = [work_b[q][:, 1024:2048].rearrange("p (s t) -> p s t", s=SH) for q in range(2)]

        x2_loaded = sem2("x2_loaded")
        slot_set = sem2("slot_set")
        tok_set = sem2("tok_set")
        first_done = sem2("first_done")
        pair_gathered = sem2("pair_gathered")
        x2T_hi = sem2("x2T_hi")
        x2T_lo = sem2("x2T_lo")
        sg_done = sem2("sg_done")
        su_done = sem2("su_done")
        ssilu_done = sem2("ssilu_done")
        shid_done = sem2("shid_done")
        sh_hi_done = sem2("sh_hi_done")
        sh_lo_done = sem2("sh_lo_done")
        sy_done = sem2("sy_done")
        two_done = sem2("two_done")
        mix_done = sem2("mix_done")
        res_done = sem2("res_done")
        res_loaded = sem2("res_loaded")
        out_stored = sem2("out_stored")

        psS, psY = [bank[2:4], bank[4:6]], bank[6:8]

        with nc.Block() as block:
            @block.sync
            def _(sp):
                def load(i, q):
                    wait_reuse(sp, x2T_hi[q], i, 1)
                    wait_reuse(sp, x2T_lo[q], i, 1)
                    sp.dma_start(x2T[q], xnT_dram[2 * i + q]).then_inc(x2_loaded[q], 16)

                def load_residual(i, q):
                    tile0 = (2 * i + q) * G
                    wait_reuse(sp, out_stored[q], i, 16)
                    sp.dma_start(res[q][:], x[bass.ds(tile0, G)].rearrange("t d n -> d t n"))\
                        .then_inc(res_loaded[q], 16)

                def store(i, q):
                    tile0 = (2 * i + q) * G
                    sp.wait_ge(res_done[q], 2 * (i + 1))
                    sp.dma_start(out[bass.ds(tile0, G)].rearrange("t d n -> d t n"), res[q][:])\
                        .then_inc(out_stored[q], 16)

                load(0, 0)
                load(0, 1)
                load_residual(0, 0)
                load_residual(0, 1)
                load(1, 0)

                def step(c):
                    i, q = c
                    if not isinstance(i, int) or 2 * i + q + 3 < NG:
                        load(i + 1 + q, 1 - q)
                    store(i, q)
                    if not isinstance(i, int) or i + 1 < NG // 2:
                        load_residual(i + 1, q)

                run_stages(sp, step, 1, NG // 2, peeled=2)
                for q in range(2):
                    sp.wait_ge(out_stored[q], 16 * (NG // 2))

            @block.gpsimd
            def _(pool):
                def step(i, q):
                    wait_reuse(pool, mix_done[q], i, 1)
                    pool.wait_ge(slot_set[q], i + 1)
                    pass_waits(pool, passed["pool"])
                    for k in range(K2):
                        pool.indirect_dma_start(
                            out=pair_rows[q][:, k, :], out_offset=None, in_=y_dram,
                            in_offset=bass.IndirectOffsetOnAxis(ap=slot_now[q][:, k:k + 1], axis=0))\
                            .then_inc(pair_gathered[q], 16)

                run_pairs(pool, step, NG // 2)

            @block.scalar
            def _(act):
                for q in range(2):
                    act.activation(slot_now[q][:], slot_all[:, q, :], ACT.Copy).then_inc(slot_set[q], 1)

                def step(a, bb, c):
                    if c:
                        i, q = c
                        act.wait_ge(pair_gathered[q], 16 * K2 * (i + 1))
                        if not isinstance(i, int) or i + 1 < NG // 2:
                            act.activation(slot_now[q][:], slot_all[:, 2 * i + 2 + q, :], ACT.Copy)\
                                .then_inc(slot_set[q], 1)
                        wait_reuse(act, two_done[q], i, G)
                        act.activation(tok_now[q][:], tok_all[:, 2 * i + q], ACT.Copy).then_inc(tok_set[q], 1)
                        act.wait_ge(tok_set[q], i + 1)
                        for t in range(G):
                            act.activation(pair_rows[q][:, TOPK * t, :], pair_rows[q][:, TOPK * t, :],
                                           ACT.Identity, bias=tok_now[q][:, 2, t:t + 1],
                                           scale=tok_now[q][:, 3, t:t + 1]).then_inc(first_done[q], 1)
                    if a:
                        i, q = a
                        act.wait_ge(x2_loaded[q], 16 * (i + 1))
                        wait_reuse(act, su_done[q], i, SH)
                        act.activation(xT_hi[q][:].rearrange("p c t -> p (c t)"), x2T[q], ACT.Copy)\
                            .then_inc(x2T_hi[q], 1)
                    if bb:
                        i, q = bb
                        wait_reuse(act, shid_done[q], i, SH)
                        for s in range(SH):
                            act.wait_ge(sg_done[q], SH * i + s + 1)
                            act.activation(s_silu[q][:, s, :], psS[s][0][:], ACT.Silu).then_inc(ssilu_done[q], 1)
                    if bb:
                        i, q = bb
                        wait_reuse(act, sy_done[q], i, 2)
                        for s in range(SH):
                            act.wait_ge(shid_done[q], SH * i + s + 1)
                            act.activation(h_hi[q][:, s], s_hid[q][:, s, :], ACT.Copy).then_inc(sh_hi_done[q], 1)

                run_stages(act, step, 3, NG // 2)

            @block.vector
            def _(dve):
                def step(a, bb, c):
                    if c:
                        i, q = c
                        dve.wait_ge(tok_set[q], i + 1)
                        for t in range(G):
                            dve.wait_ge(first_done[q], G * i + t + 1)
                            dve.scalar_tensor_tensor(pair_rows[q][:, TOPK * t, :],
                                                     pair_rows[q][:, TOPK * t + 1, :],
                                                     tok_now[q][:, 4, t:t + 1], pair_rows[q][:, TOPK * t, :],
                                                     ALU.mult, ALU.add).then_inc(two_done[q], 1)
                        dve.wait_ge(res_loaded[q], 16 * (i + 1))
                        dve.wait_ge(two_done[q], G * (i + 1))
                        dve.tensor_tensor(res[q][:], res[q][:], pair_rows[q][:, 0::TOPK, :], ALU.add)\
                            .then_inc(mix_done[q], 1)
                    if bb:
                        i, q = bb
                        wait_reuse(dve, sh_lo_done[q], i, SH)
                        wait_reuse(dve, sh_hi_done[q], i, SH)
                        for s in range(SH):
                            dve.wait_ge(ssilu_done[q], SH * i + s + 1)
                            dve.wait_ge(su_done[q], SH * i + s + 1)
                            dve.tensor_tensor(s_hid[q][:, s, :], s_silu[q][:, s, :], psS[s][1][:], ALU.mult)\
                                .then_inc(shid_done[q], 1)
                    if a:
                        i, q = a
                        wait_reuse(dve, su_done[q], i, SH)
                        dve.wait_ge(x2T_hi[q], i + 1)
                        dve.tensor_tensor(xT_lo[q][:].rearrange("p c t -> p (c t)"), x2T[q],
                                          xT_hi[q][:].rearrange("p c t -> p (c t)").bitcast(F32),
                                          ALU.subtract).then_inc(x2T_lo[q], 1)
                    if bb:
                        i, q = bb
                        wait_reuse(dve, sy_done[q], i, 2)
                        for s in range(SH):
                            dve.wait_ge(sh_hi_done[q], SH * i + s + 1)
                            dve.tensor_tensor(h_lo[q][:, s], s_hid[q][:, s, :], h_hi[q][:, s].bitcast(F32),
                                              ALU.subtract).then_inc(sh_lo_done[q], 1)
                    if c:
                        i, q = c
                        for j in range(2):
                            dve.wait_ge(sy_done[q], 2 * i + j + 1)
                            dve.wait_ge(mix_done[q], i + 1)
                            half = res[q][:, 2 * j:2 * j + 2, :].rearrange("p t n -> p (t n)")
                            dve.tensor_tensor(half, half, psY[j][:], ALU.add).then_inc(res_done[q], 1)

                run_stages(dve, step, 3, NG // 2)

            @block.tensor
            def _(pe):
                def step(a, bb, c):
                    if bb:
                        i, q = bb
                        pe.wait_ge(x2T_hi[q], i + 1)
                        pe.wait_ge(x2T_lo[q], i + 1)
                        wait_before(pe, ssilu_done, bb, SH)
                        wait_before(pe, shid_done, bb, SH)
                        for s in range(SH):
                            for k, done in enumerate((sg_done, su_done)):
                                three_passes(pe, psS[s][k][:], [
                                    ((sw13_hi[:, k, ch, s], sw13_lo[:, k, ch, s]),
                                     (xT_hi[q][:, ch], xT_lo[q][:, ch])) for ch in range(C)]).then_inc(done[q], 1)
                    if c:
                        i, q = c
                        pe.wait_ge(sh_hi_done[q], SH * (i + 1))
                        pe.wait_ge(sh_lo_done[q], SH * (i + 1))
                        wait_before(pe, res_done, c, 2)
                        for j in range(2):
                            for t in (2 * j, 2 * j + 1):
                                last = three_passes(pe, psY[j][:, t % 2 * N:(t % 2 + 1) * N], [
                                    ((h_hi[q][:, s, t * P:(t + 1) * P], h_lo[q][:, s, t * P:(t + 1) * P]),
                                     (sw2_hi[:, s], sw2_lo[:, s])) for s in range(SH)])
                            last.then_inc(sy_done[q], 1)

                run_stages(pe, step, 3, NG // 2)


_INS = ['x', 'adj', 'L0_gnn_b', 'L0_ffn_gate_w', 'L0_ffn_w1', 'L0_ffn_w3', 'L0_ffn_w2', 'L0_ffn_sw1', 'L0_ffn_sw3',
        'L0_ffn_sw2']
_OUTS = [((128, 128, 256), 'float32')]


def kernel(**inputs):
    import numpy as _np
    import concourse.bacc as _bacc
    from concourse import mybir as _mybir
    from concourse.bass_utils import run_bass_kernel_spmd as _run

    nc = _bacc.Bacc("TRN2", target_bir_lowering=False, num_devices=1)
    arrays, args = {}, []
    for name in _INS:
        a = _np.ascontiguousarray(inputs[name])
        arrays[f"in_{name}_dram"] = a
        args.append(nc.dram_tensor(f"in_{name}_dram", a.shape, _mybir.dt.from_np(a.dtype), kind="ExternalInput").ap())
    for i, (shape, dtype) in enumerate(_OUTS):
        dt = _mybir.dt.from_np(_np.dtype(dtype))
        args.append(nc.dram_tensor(f"out_{i}_dram", shape, dt, kind="ExternalOutput").ap())
    build(nc, *args)
    r = _run(nc, [arrays], core_ids=[0])
    return r.results[0]["out_0_dram"]
```

```python
import concourse.bass as bass
from concourse import mybir
from contextlib import ExitStack


F32 = mybir.dt.float32
F32R = mybir.dt.float32r
BF16 = mybir.dt.bfloat16
FP16 = mybir.dt.float16
U32 = mybir.dt.uint32
ACT = mybir.ActivationFunctionType
ALU = mybir.AluOpType
AX = mybir.AxisListType

P = 128
CAP = 512
TOPK = 2
ROUTE_SCALE = 2.5
EPS = 1e-5
G = 4
REC = 7 * G


def run_stages(engine, step, depth, pairs, peeled=1):
    def items(j, r, known):
        at = []
        for d in range(depth):
            q = (r - d) % 2
            i = j + (r - d - q) // 2
            at.append((i, q) if not known or 0 <= i < pairs else None)
        return at

    first = (depth + 2) // 2
    for n in range(2 * first):
        step(*items(0, n, True))
    with engine.Fori(first, pairs - peeled) as j:
        for r in range(2):
            step(*items(j, r, False))
    for n in range(2 * (pairs - peeled), 2 * pairs + depth - 1):
        step(*items(0, n, True))


def run_pairs(engine, step, pairs):
    for q in range(2):
        step(0, q)
    with engine.Fori(1, pairs) as i:
        for q in range(2):
            step(i, q)


def wait_before(engine, sems, at, n):
    i, q = at
    if q == 1:
        engine.wait_ge(sems[0], (i + 1) * n)
    elif not (isinstance(i, int) and i == 0):
        engine.wait_ge(sems[1], i * n)


def wait_reuse(engine, sem, i, n):
    if not (isinstance(i, int) and i == 0):
        engine.wait_ge(sem, i * n)


def pass_waits(engine, passed):
    engine.sem_inc(passed, 1)


def build(nc, x, adj, b, gate_w, w1, w3, w2, sw1, sw3, sw2, out):
    B, D, N = x.shape
    E, _, H = w1.shape
    SH = sw1.shape[1] // P
    C = N // P
    S = CAP // P
    NG = B // G
    K2 = G * TOPK
    assert D == P and H == P and S == G and C == 2 and SH == 2 and 2 * E == P

    xn_dram = nc.dram_tensor("xn_rows", [B * D, N], F32, kind="Internal").ap()
    xnT_dram = nc.dram_tensor("xn_columns", [NG, P, C * 512], F32, kind="Internal").ap()
    y_dram = nc.dram_tensor("slot_rows", [E * CAP, N], F32, kind="Internal").ap()

    ctx = ExitStack()
    with ctx:
        def sb(name, shape, dt):
            return ctx.enter_context(nc.sbuf_tensor(name, shape, dt))

        def sb2(name, shape, dt):
            return [sb(f"{name}{q}", shape, dt) for q in range(2)]

        def sem(name):
            return ctx.enter_context(nc.semaphore(name))

        def sem2(name):
            return [sem(f"{name}{q}") for q in range(2)]

        passed = {engine: sem(f"passed_{engine}") for engine in ("pool", "dve", "pe")}

        bank = [ctx.enter_context(nc.psum_tensor(f"bank{k}", [P, 512], F32)) for k in range(8)]

        ident = sb("ident", [P, P], F32)
        ones = sb("ones", [P, P], BF16)
        before = sb("before", [P, P], BF16)
        zero = sb("zero", [P, 512], BF16)
        slot_iota = sb("slot_iota", [P, CAP], FP16)
        expert_iota = sb("expert_iota", [P, E], F32)
        part_iota = sb("part_iota", [P, 1], F32)
        tile_iota = sb("tile_iota", [P, B], F32)
        minus_half = sb("minus_half", [P, G], F32)
        minus_one = sb("minus_one", [P, G], F32)
        eps = sb("eps", [P, G], F32)
        join = sb("join", [P, E], BF16)
        adj_raw = sb("adj_raw", [P, P], F32)
        adjT = sb("adjT", [P, P], F32)
        gate_raw = sb("gate_raw", [E, N], F32)
        gateT = sb("gateT", [P, C, E], F32)
        bias = sb("bias", [P, 1], F32)
        rec_all = sb("rec_all", [P, NG, REC], F32)
        tok_all = sb("tok_all", [P, NG, 3, G], F32)
        slot_all = sb("slot_all", [P, NG, K2], U32)
        token_of = sb("token_of", [P, E, S], U32)

        x_in = sb2("x_in", [P, G, N], F32)
        xn = sb2("xn", [P, G, N], F32)
        xT_hi = sb2("xT_hi", [P, C, 512], F32R)
        xT_lo = sb2("xT_lo", [P, C, 512], F32R)
        work_a = sb2("work_a", [P, 4096], F32)
        work_b = sb2("work_b", [P, 2048], F32)

        res = sb2("res", [P, G, N], F32)
        sw13_hi = sb("sw13_hi", [P, 2, C, SH, P], F32R)
        sw13_lo = sb("sw13_lo", [P, 2, C, SH, P], F32R)
        sw2_hi = sb("sw2_hi", [P, SH, N], F32R)
        sw2_lo = sb("sw2_lo", [P, SH, N], F32R)
        sw13_raw = res[0][:].rearrange("p t n -> p (t n)").rearrange("p (w n) -> p w n", w=2)
        sw2_raw = res[1][:, 0:SH, :]
        sw_loaded = sem("sw_loaded")
        sw_hi_done = sem("sw_hi_done")
        sw_lo_done = sem("sw_lo_done")

        stats = sb2("stats", [P, G, 6], F32)
        mv = sb2("mv", [P, G, 2], F32)
        var_eps = sb2("var_eps", [P, G], F32)
        norm = sb2("norm", [P, 2, G], F32)
        neg_mean = sb2("neg_mean", [P, G], F32)
        xT = [work_b[q][:, 0:C * 512].rearrange("p (c t) -> p c t", c=C) for q in range(2)]
        score = [work_b[q][:, 1536:1536 + G * E].rearrange("p (t e) -> p t e", t=G) for q in range(2)]
        top8 = sb2("top8", [P, G, 8], F32)
        idx8 = sb2("idx8", [P, G, 8], U32)
        rec = sb2("rec", [P, K2 + G], F32)
        onehot = sb2("onehot", [P, G, TOPK, E], BF16)
        mask = sb2("mask", [P, G, E], BF16)
        seen = sb2("seen", [P, G, E], BF16)
        tagged = sb2("tagged", [P, K2, 2, E], BF16)
        prefix = sb2("prefix", [P, G * E], F32)
        pos_junk = sb("pos_junk", [P, K2, E], F32)
        posdot = sb("posdot", [P, K2, E], F32)
        at_pos = [work_a[q][:, 0:2048].bitcast(BF16).rearrange("p (k s) -> p k s", k=K2) for q in range(2)]

        s_const = sem("s_const")
        s_raw = [sem(f"s_raw{k}") for k in range(3)]
        s_wT = sem("s_wT")
        s_wTc = sem("s_wTc")
        x_loaded = sem2("x_loaded")
        mv_done = sem2("mv_done")
        norm_step = sem2("norm_step")
        ln_done = sem2("ln_done")
        xn_stored = sem2("xn_stored")
        xnT_done = sem2("xnT_done")
        xT_done = sem2("xT_done")
        xT_stored = sem2("xT_stored")
        gate_done = sem2("gate_done")
        score_done = sem2("score_done")
        gnn_done = sem2("gnn_done")
        gmax_done = sem2("gmax_done")
        idx_done = sem2("idx_done")
        onehot_done = sem2("onehot_done")
        mask_done = sem2("mask_done")
        seen_done = sem2("seen_done")
        tagged_done = sem2("tagged_done")
        prefix_done = sem2("prefix_done")
        prefix_copied = sem2("prefix_copied")
        posdot_done = sem2("posdot_done")
        pos_done = sem2("pos_done")
        at_done = sem2("at_done")
        table_done = sem2("table_done")
        rec_saved = sem2("rec_saved")
        s_table = sem("s_table")
        s_tabc = sem("s_tabc")
        s_join = sem("s_join")
        tokens_done = sem("tokens_done")
        fin_done = sem("fin_done")
        s_fin = sem("s_fin")

        table = work_a[0][:, 0:CAP // 2].bitcast(BF16)
        psT, psA, psL, psP, psTab = bank[0:2], bank[3:5], bank[5], bank[6], bank[7]

        w13_raw = [work_a[q][:, 2048:2560].rearrange("p (w c h) -> p w c h", w=2, c=C) for q in range(2)]
        w2_raw = [work_a[q][:, 2560:2816] for q in range(2)]
        w13_hi = sb2("w13_hi", [P, 2, C, H], F32R)
        w13_lo = sb2("w13_lo", [P, 2, C, H], F32R)
        w2_hi = sb2("w2_hi", [P, N], F32R)
        w2_lo = sb2("w2_lo", [P, N], F32R)
        rows = xn
        token_now = sb2("token_now", [P, S], U32)
        silu = [work_b[q][:, 0:512] for q in range(2)]
        hid = [work_b[q][:, 512:1024] for q in range(2)]
        h_hi = sb2("h_hi", [P, SH, 512], F32R)
        h_lo = sb2("h_lo", [P, SH, 512], F32R)
        y_out = x_in

        w13_loaded = sem2("w13_loaded")
        w2_loaded = sem2("w2_loaded")
        w13_hi_done = sem2("w13_hi_done")
        w13_lo_done = sem2("w13_lo_done")
        w2_hi_done = sem2("w2_hi_done")
        w2_lo_done = sem2("w2_lo_done")
        token_set = sem2("token_set")
        gathered = sem2("gathered")
        rowsT_done = sem2("rowsT_done")
        rT_hi_done = sem2("rT_hi_done")
        rT_lo_done = sem2("rT_lo_done")
        g_done = sem2("g_done")
        u_done = sem2("u_done")
        silu_done = sem2("silu_done")
        hid_done = sem2("hid_done")
        h_hi_done = sem2("h_hi_done")
        h_lo_done = sem2("h_lo_done")
        y_done = sem2("y_done")
        y_act = sem2("y_act")
        y_dve = sem2("y_dve")
        y_stored = sem2("y_stored")

        def three_passes(pe, ps, terms):
            products = [(wv, mv_) for (w_hi, w_lo), (m_hi, m_lo) in terms
                        for wv, mv_ in ((w_hi, m_hi), (w_hi, m_lo), (w_lo, m_hi))]
            for n, (wv, mv_) in enumerate(products):
                last = pe.matmul(ps, wv, mv_, start=(n == 0), stop=(n == len(products) - 1))
            return last

        psT, psGU, psY = bank[0:2], [bank[2:4], bank[4:6]], bank[6:8]

        pair_rows = [work_a[q][:, 0:K2 * N].rearrange("p (k n) -> p k n", k=K2) for q in range(2)]
        x2T = [xn[q][:].rearrange("p t n -> p (t n)") for q in range(2)]
        slot_now = sb2("slot_now", [P, K2], U32)
        tok_now = sb2("tok_now", [P, 3, G], F32)
        s_silu = [work_b[q][:, 0:1024].rearrange("p (s t) -> p s t", s=SH) for q in range(2)]
        s_hid = [work_b[q][:, 1024:2048].rearrange("p (s t) -> p s t", s=SH) for q in range(2)]

        x2_loaded = sem2("x2_loaded")
        slot_set = sem2("slot_set")
        tok_set = sem2("tok_set")
        first_done = sem2("first_done")
        pair_gathered = sem2("pair_gathered")
        x2T_hi = sem2("x2T_hi")
        x2T_lo = sem2("x2T_lo")
        sg_done = sem2("sg_done")
        su_done = sem2("su_done")
        ssilu_done = sem2("ssilu_done")
        shid_done = sem2("shid_done")
        sh_hi_done = sem2("sh_hi_done")
        sh_lo_done = sem2("sh_lo_done")
        sy_done = sem2("sy_done")
        two_done = sem2("two_done")
        mix_done = sem2("mix_done")
        res_done = sem2("res_done")
        res_loaded = sem2("res_loaded")
        out_stored = sem2("out_stored")

        psS, psY = [bank[2:4], bank[4:6]], bank[6:8]

        with nc.Block() as block:
            @block.sync
            def _(sp):
                def load(i, q):
                    tile0 = (2 * i + q) * G
                    sp.dma_start(x_in[q][:], x[bass.ds(tile0, G)].rearrange("t d n -> d t n"))\
                        .then_inc(x_loaded[q], 16)

                def store(i, q):
                    sp.wait_ge(ln_done[q], G * (i + 1))
                    row0 = (2 * i + q) * G * D
                    sp.dma_start(xn_dram[bass.ds(row0, G * D)].rearrange("(t d) n -> d t n", t=G), xn[q][:])\
                        .then_inc(xn_stored[q], 16)

                def store_T(i, q):
                    sp.wait_ge(xT_done[q], C * (i + 1))
                    sp.dma_start(xnT_dram[2 * i + q], xT[q].rearrange("p c t -> p (c t)"))\
                        .then_inc(xT_stored[q], 16)

                def step(z, a):
                    if z:
                        i, q = z
                        if not isinstance(i, int) or i + 1 < NG // 2:
                            sp.wait_ge(ln_done[q], G * (i + 1))
                            load(i + 1, q)
                        store(i, q)
                    if a:
                        store_T(*a)

                load(0, 0)
                load(0, 1)
                sp.dma_start(adj_raw[:], adj).then_inc(s_raw[0], 16)
                sp.dma_start(gate_raw[:], gate_w).then_inc(s_raw[1], 16)
                sp.dma_start(bias[:], b.rearrange("(d a) -> d a", a=1)).then_inc(s_raw[2], 16)
                for k, w in enumerate((sw1, sw3)):
                    sp.dma_start(sw13_raw[:, k],
                                 w.rearrange("(p c) h -> p (c h)", c=C)).then_inc(sw_loaded, 16)
                sp.dma_start(sw2_raw, sw2.rearrange("(s p) n -> p s n", s=SH)).then_inc(sw_loaded, 16)
                run_stages(sp, step, 2, NG // 2)

                def load_up(i, q):
                    e = 2 * i + q
                    wait_reuse(sp, w13_lo_done[q], i, 1)
                    wait_reuse(sp, w13_hi_done[q], i, 1)
                    for k, w in enumerate((w1, w3)):
                        sp.dma_start(w13_raw[q][:, k].rearrange("p c h -> p (c h)"),
                                     w[e].rearrange("(p c) h -> p (c h)", c=C)).then_inc(w13_loaded[q], 16)

                def load_down(i, q):
                    e = 2 * i + q
                    wait_reuse(sp, w2_lo_done[q], i, 1)
                    wait_reuse(sp, w2_hi_done[q], i, 1)
                    sp.dma_start(w2_raw[q], w2[e]).then_inc(w2_loaded[q], 16)

                def store(i, q):
                    sp.wait_ge(y_act[q], i + 1)
                    sp.wait_ge(y_dve[q], i + 1)
                    row0 = (2 * i + q) * CAP
                    sp.dma_start(y_dram[bass.ds(row0, CAP)].rearrange("(p s) n -> p (s n)", s=S),
                                 y_out[q][:].rearrange("p s n -> p (s n)")).then_inc(y_stored[q], 16)

                def first_loads():
                    for q in range(2):
                        sp.wait_ge(xT_stored[q], 16 * (NG // 2))
                        sp.wait_ge(rowsT_done[q], C * (E // 2))
                        sp.dma_start(x2T[q], xnT_dram[q]).then_inc(x2_loaded[q], 16)

                def step(a, bb, c):
                    if a:
                        i, q = a
                        if not isinstance(i, int) or i + 1 < E // 2:
                            load_up(i + 1, q)
                            load_down(i + q, 1 - q)
                        elif q == 0:
                            load_down(i, 1)
                    if bb and not a:
                        first_loads()
                    if c:
                        store(*c)

                load_up(0, 0)
                load_up(0, 1)
                load_down(0, 0)
                run_stages(sp, step, 3, E // 2)

                def load(i, q):
                    wait_reuse(sp, x2T_hi[q], i, 1)
                    wait_reuse(sp, x2T_lo[q], i, 1)
                    sp.dma_start(x2T[q], xnT_dram[2 * i + q]).then_inc(x2_loaded[q], 16)

                def load_residual(i, q):
                    tile0 = (2 * i + q) * G
                    wait_reuse(sp, out_stored[q], i, 16)
                    sp.dma_start(res[q][:], x[bass.ds(tile0, G)].rearrange("t d n -> d t n"))\
                        .then_inc(res_loaded[q], 16)

                def store(i, q):
                    tile0 = (2 * i + q) * G
                    sp.wait_ge(res_done[q], 2 * (i + 1))
                    sp.dma_start(out[bass.ds(tile0, G)].rearrange("t d n -> d t n"), res[q][:])\
                        .then_inc(out_stored[q], 16)

                sp.wait_ge(sw_hi_done, 2)
                sp.wait_ge(sw_lo_done, 2)
                load_residual(0, 0)
                load_residual(0, 1)
                load(1, 0)

                def step(c):
                    i, q = c
                    if not isinstance(i, int) or 2 * i + q + 3 < NG:
                        load(i + 1 + q, 1 - q)
                    store(i, q)
                    if not isinstance(i, int) or i + 1 < NG // 2:
                        load_residual(i + 1, q)

                run_stages(sp, step, 1, NG // 2, peeled=2)
                for q in range(2):
                    sp.wait_ge(xn_stored[q], 16 * (NG // 2))
                    sp.wait_ge(y_stored[q], 16 * (E // 2))
                    sp.wait_ge(out_stored[q], 16 * (NG // 2))

            @block.gpsimd
            def _(pool):
                pool.memset(ident[:], 0.0).then_inc(s_const, 1)
                pool.memset(before[:], 1.0).then_inc(s_const, 1)
                pool.memset(join[:], 0.0).then_inc(s_const, 1)
                pool.memset(ones[:], 1.0).then_inc(s_const, 1)
                pool.memset(zero[:], 0.0).then_inc(s_const, 1)
                pool.memset(minus_half[:], -0.5).then_inc(s_const, 1)
                pool.memset(minus_one[:], -1.0).then_inc(s_const, 1)
                pool.memset(eps[:], EPS).then_inc(s_const, 1)
                pool.memset(seen[0][:, 0, :], 0.0).then_inc(s_const, 1)
                pool.iota(slot_iota[:], [[1, CAP]], base=0, channel_multiplier=0,
                          allow_small_or_imprecise_dtypes=True).then_inc(s_const, 1)
                pool.iota(expert_iota[:], [[1, E]], base=0, channel_multiplier=0,
                          allow_small_or_imprecise_dtypes=True).then_inc(s_const, 1)
                pool.iota(part_iota[:], [[0, 1]], base=0, channel_multiplier=1,
                          allow_small_or_imprecise_dtypes=True).then_inc(s_const, 1)
                pool.iota(tile_iota[:], [[1, B]], base=0, channel_multiplier=0,
                          allow_small_or_imprecise_dtypes=True).then_inc(s_const, 1)
                pool.wait_ge(s_const, 13)
                pool.affine_select(out=ident[:], in_=ident[:], compare_op=ALU.not_equal, fill=1.0, base=0,
                                   pattern=[[-1, P]], channel_multiplier=1).then_inc(s_const, 1)
                pool.affine_select(out=before[:], in_=before[:], compare_op=ALU.is_gt, fill=0.0, base=0,
                                   pattern=[[1, P]], channel_multiplier=-1).then_inc(s_const, 1)
                pool.affine_select(out=join[:], in_=join[:], compare_op=ALU.not_equal, fill=1.0, base=0,
                                   pattern=[[-1, E]], channel_multiplier=1).then_inc(s_const, 1)
                pool.wait_ge(s_const, 16)
                pool.affine_select(out=join[:], in_=join[:], compare_op=ALU.not_equal, fill=float(P), base=-E,
                                   pattern=[[-1, E]], channel_multiplier=1).then_inc(s_const, 1)

                def step(z, a, bb, c):
                    if c:
                        i, q = c
                        pool.wait_ge(prefix_copied[q], i + 1)
                        pool.wait_ge(onehot_done[q], i + 1)
                        wait_before(pool, pos_done, c, K2)
                        pool.tensor_tensor(
                            posdot[:].rearrange("p (t k) e -> p t k e", k=TOPK), onehot[q][:],
                            prefix[q][:].rearrange("p (t e) -> p t e", t=G).unsqueeze(2)
                            .to_broadcast([P, G, TOPK, E]), ALU.mult).then_inc(posdot_done[q], 1)
                    if z:
                        i, q = z
                        pool.wait_ge(mv_done[q], 2 * G * (i + 1))
                        wait_reuse(pool, ln_done[q], i, G)
                        pool.tensor_tensor(var_eps[q][:], mv[q][:, :, 1], eps[:], ALU.add)\
                            .then_inc(norm_step[q], 1)
                        pool.tensor_tensor(neg_mean[q][:], mv[q][:, :, 0], minus_one[:], ALU.mult)\
                            .then_inc(norm_step[q], 1)
                        pool.wait_ge(norm_step[q], 4 * i + 1)
                        pool.tensor_tensor(norm[q][:, 0, :], var_eps[q][:], minus_half[:], ALU.pow)\
                            .then_inc(norm_step[q], 1)
                        pool.wait_ge(norm_step[q], 4 * i + 3)
                        pool.tensor_tensor(norm[q][:, 1, :], neg_mean[q][:], norm[q][:, 0, :], ALU.mult)\
                            .then_inc(norm_step[q], 1)
                    if bb:
                        i, q = bb
                        oh = onehot[q][:].rearrange("p t k e -> p (t k) e")
                        pool.wait_ge(onehot_done[q], i + 1)
                        wait_reuse(pool, prefix_done[q], i, 1)
                        pool.tensor_tensor(mask[q][:], onehot[q][:, :, 0, :], onehot[q][:, :, 1, :], ALU.add)\
                            .then_inc(mask_done[q], 1)
                        pool.wait_ge(mask_done[q], i + 1)
                        for t in range(1, G):
                            pool.tensor_tensor(seen[q][:, t, :], seen[q][:, t - 1, :], mask[q][:, t - 1, :],
                                               ALU.add).then_inc(seen_done[q], 1)
                            pool.wait_ge(seen_done[q], G * i + t)
                        wait_before(pool, prefix_done, bb, 1)
                        pool.tensor_tensor(seen[1 - q][:, 0, :], seen[q][:, G - 1, :], mask[q][:, G - 1, :],
                                           ALU.add).then_inc(seen_done[q], 1)
                        wait_reuse(pool, table_done[q], i, 1)
                        pass_waits(pool, passed["pool"])
                        pool.tensor_scalar(tagged[q][:, :, 0, :], oh, part_iota[:, 0:1], 1.0, ALU.mult, ALU.mult)\
                            .then_inc(tagged_done[q], 1)
                        group = 2 * i + q
                        pool.tensor_tensor(
                            tagged[q][:, :, 1, :].rearrange("p (t k) e -> p t k e", k=TOPK), onehot[q][:],
                            tile_iota[:, bass.ds(group * G, G)].unsqueeze(2).unsqueeze(3)
                            .to_broadcast([P, G, TOPK, E]), ALU.mult).then_inc(tagged_done[q], 1)
                        pool.wait_ge(seen_done[q], G * (i + 1))

                run_stages(pool, step, 4, NG // 2)

                def step(i, q):
                    if isinstance(i, int) and i == 0:
                        pool.wait_ge(tokens_done, 1)
                    else:
                        pool.wait_ge(token_set[q], i)
                    now = token_of[:, q, :] if isinstance(i, int) and i == 0 else token_now[q][:]
                    wait_reuse(pool, rowsT_done[q], i, C)
                    pass_waits(pool, passed["pool"])
                    for s in range(S):
                        pool.indirect_dma_start(
                            out=rows[q][:, s, :], out_offset=None, in_=xn_dram,
                            in_offset=bass.IndirectOffsetOnAxis(ap=now[:, s:s + 1], axis=0))\
                            .then_inc(gathered[q], 16)

                for q in range(2):
                    pool.wait_ge(xn_stored[q], 16 * (NG // 2))
                    pool.wait_ge(gnn_done[q], G // 2 * (NG // 2))
                run_pairs(pool, step, E // 2)

                def step(i, q):
                    wait_reuse(pool, mix_done[q], i, 1)
                    pool.wait_ge(slot_set[q], i + 1)
                    pass_waits(pool, passed["pool"])
                    for k in range(K2):
                        pool.indirect_dma_start(
                            out=pair_rows[q][:, k, :], out_offset=None, in_=y_dram,
                            in_offset=bass.IndirectOffsetOnAxis(ap=slot_now[q][:, k:k + 1], axis=0))\
                            .then_inc(pair_gathered[q], 16)

                for q in range(2):
                    pool.wait_ge(y_stored[q], 16 * (E // 2))
                run_pairs(pool, step, NG // 2)

            @block.scalar
            def _(act):
                act.wait_ge(s_wT, 2)
                act.activation(adjT[:], psA[0][:, 0:P], ACT.Copy).then_inc(s_wTc, 1)
                act.activation(gateT[:].rearrange("p c e -> p (c e)"), psA[1][:, 0:C * E], ACT.Copy)\
                    .then_inc(s_wTc, 1)

                def step(z, a, bb, c):
                    if c:
                        i, q = c
                        act.wait_ge(prefix_done[q], i + 1)
                        wait_reuse(act, posdot_done[q], i, 1)
                        act.activation(prefix[q][:], psP[:, 0:G * E], ACT.Copy).then_inc(prefix_copied[q], 1)
                    if a:
                        i, q = a
                        wait_reuse(act, xT_stored[q], i, 16)
                        wait_reuse(act, gate_done[q], i, 1)
                        for ch in range(C):
                            act.wait_ge(xnT_done[q], C * i + ch + 1)
                            act.activation(xT[q][:, ch, :], psT[ch][:], ACT.Copy).then_inc(xT_done[q], 1)
                    if c:
                        i, q = c
                        act.wait_ge(posdot_done[q], i + 1)
                        for k in range(K2):
                            act.activation(pos_junk[:, k], posdot[:, k, :], ACT.Copy,
                                           accum_out=rec[q][:, k:k + 1])\
                                .then_inc(pos_done[q], 1)
                        act.wait_ge(gmax_done[q], G // 2 * (i + 1))
                        act.wait_ge(idx_done[q], 2 * G * (i + 1))
                        act.wait_ge(pos_done[q], K2 * (i + 1))
                        for at, part in ((0, top8), (K2, idx8)):
                            act.activation(
                                rec_all[:, 2 * i + q, at:at + K2].rearrange("p (t k) -> p t k", k=TOPK),
                                part[q][:, :, 0:TOPK], ACT.Copy).then_inc(rec_saved[q], 1)
                        act.activation(rec_all[:, 2 * i + q, 2 * K2:REC], rec[q][:], ACT.Copy)\
                            .then_inc(rec_saved[q], 1)
                    if z:
                        i, q = z
                        act.wait_ge(norm_step[q], 4 * (i + 1))
                        act.wait_ge(x_loaded[q], 16 * (i + 1))
                        wait_reuse(act, xn_stored[q], i, 16)
                        wait_reuse(act, gnn_done[q], i, G // 2)
                        for t in range(G):
                            act.activation(xn[q][:, t, :], x_in[q][:, t, :], ACT.Identity,
                                           bias=norm[q][:, 1, t:t + 1], scale=norm[q][:, 0, t:t + 1])\
                                .then_inc(ln_done[q], 1)
                    if a:
                        i, q = a
                        act.wait_ge(gate_done[q], i + 1)
                        wait_reuse(act, idx_done[q], i, 2 * G)
                        act.activation(score[q], psL[:, 0:G * E].rearrange("p (t e) -> p t e", t=G),
                                       ACT.Sigmoid).then_inc(score_done[q], 1)

                run_stages(act, step, 4, NG // 2)
                act.wait_ge(s_table, 1)
                wait_before(act, at_done, (NG // 2, 0), K2)
                act.activation(table, psTab[:], ACT.Copy).then_inc(s_tabc, 1)

                def set_tokens(i, q):
                    act.activation(token_now[q][:], token_of[:, 2 * i + q, :], ACT.Copy)\
                        .then_inc(token_set[q], 1)

                act.wait_ge(tokens_done, 1)
                set_tokens(1, 0)
                set_tokens(1, 1)
                act.wait_ge(sw_loaded, 48)
                act.activation(sw13_hi[:].rearrange("p w c s h -> p w (c s h)"), sw13_raw, ACT.Copy)\
                    .then_inc(sw_hi_done, 1)
                act.activation(sw2_hi[:], sw2_raw, ACT.Copy).then_inc(sw_hi_done, 1)
                for q in range(2):
                    act.wait_ge(xT_stored[q], 16 * (NG // 2))

                def step(a, bb, c):
                    if a:
                        i, q = a
                        if not isinstance(i, int) or 0 < i < E // 2 - 1:
                            act.wait_ge(gathered[q], 16 * S * (i + 1))
                            set_tokens(i + 1, q)
                        wait_reuse(act, u_done[q], i, 1)
                        for ch in range(C):
                            act.wait_ge(rowsT_done[q], C * i + ch + 1)
                            act.activation(xT_hi[q][:, ch], psT[ch][:], ACT.Copy).then_inc(rT_hi_done[q], 1)
                    if bb:
                        i, q = bb
                        act.wait_ge(g_done[q], i + 1)
                        wait_reuse(act, hid_done[q], i, 1)
                        act.activation(silu[q], psGU[q][0][:], ACT.Silu).then_inc(silu_done[q], 1)
                    if a:
                        i, q = a
                        act.wait_ge(w13_loaded[q], 32 * (i + 1))
                        act.activation(w13_hi[q][:], w13_raw[q], ACT.Copy).then_inc(w13_hi_done[q], 1)
                    if bb:
                        i, q = bb
                        wait_reuse(act, y_done[q], i, 2)
                        act.wait_ge(w2_loaded[q], 16 * (i + 1))
                        act.activation(w2_hi[q][:], w2_raw[q], ACT.Copy).then_inc(w2_hi_done[q], 1)
                        act.wait_ge(hid_done[q], i + 1)
                        act.activation(h_hi[q][:, 0], hid[q], ACT.Copy).then_inc(h_hi_done[q], 1)
                    if c:
                        i, q = c
                        act.wait_ge(y_done[q], 2 * i + 1)
                        wait_reuse(act, y_stored[q], i, 16)
                        act.activation(y_out[q][:, 0:2, :].rearrange("p s n -> p (s n)"), psY[0][:], ACT.Copy)\
                            .then_inc(y_act[q], 1)

                run_stages(act, step, 3, E // 2)

                for q in range(2):
                    act.wait_ge(fin_done, 1)
                    act.wait_ge(u_done[q], E // 2)
                    act.wait_ge(h_lo_done[q], E // 2)
                    act.wait_ge(y_done[q], 2 * (E // 2))
                    act.activation(slot_now[q][:], slot_all[:, q, :], ACT.Copy).then_inc(slot_set[q], 1)

                def step(a, bb, c):
                    if c:
                        i, q = c
                        wait_reuse(act, two_done[q], i, G)
                        act.activation(tok_now[q][:], tok_all[:, 2 * i + q], ACT.Copy).then_inc(tok_set[q], 1)
                        act.wait_ge(tok_set[q], i + 1)
                        act.wait_ge(pair_gathered[q], 16 * K2 * (i + 1))
                        for t in range(G):
                            act.activation(pair_rows[q][:, TOPK * t, :], pair_rows[q][:, TOPK * t, :],
                                           ACT.Identity, bias=tok_now[q][:, 0, t:t + 1],
                                           scale=tok_now[q][:, 1, t:t + 1]).then_inc(first_done[q], 1)
                        if not isinstance(i, int) or i + 1 < NG // 2:
                            act.activation(slot_now[q][:], slot_all[:, 2 * i + 2 + q, :], ACT.Copy)\
                                .then_inc(slot_set[q], 1)
                    if a:
                        i, q = a
                        act.wait_ge(x2_loaded[q], 16 * (i + 1))
                        wait_reuse(act, su_done[q], i, SH)
                        act.activation(xT_hi[q][:].rearrange("p c t -> p (c t)"), x2T[q], ACT.Copy)\
                            .then_inc(x2T_hi[q], 1)
                    if bb:
                        i, q = bb
                        wait_reuse(act, shid_done[q], i, SH)
                        for s in range(SH):
                            act.wait_ge(sg_done[q], SH * i + s + 1)
                            act.activation(s_silu[q][:, s, :], psS[s][0][:], ACT.Silu).then_inc(ssilu_done[q], 1)
                        wait_reuse(act, sy_done[q], i, 2)
                        for s in range(SH):
                            act.wait_ge(shid_done[q], SH * i + s + 1)
                            act.activation(h_hi[q][:, s], s_hid[q][:, s, :], ACT.Copy).then_inc(sh_hi_done[q], 1)

                run_stages(act, step, 3, NG // 2)

            @block.vector
            def _(dve):
                def step(z, a, bb, c):
                    if z:
                        i, q = z
                        dve.wait_ge(x_loaded[q], 16 * (i + 1))
                        for t in range(G):
                            dve.bn_stats(stats[q][:, t, :], x_in[q][:, t, :]).then_inc(mv_done[q], 1)
                    if bb:
                        i, q = bb
                        wait_reuse(dve, rec_saved[q], i, 3)
                        for j in range(G // 2):
                            dve.wait_ge(gnn_done[q], G // 2 * i + j + 1)
                            dve.reduce_max(rec[q][:, K2 + 2 * j:K2 + 2 * j + 2],
                                           psA[j][:].rearrange("p (t n) -> p t n", t=2), AX.X)\
                                .then_inc(gmax_done[q], 1)
                        dve.wait_ge(score_done[q], i + 1)
                        pass_waits(dve, passed["dve"])
                        for t in range(G):
                            dve.max(top8[q][:, t, :], score[q][:, t, :]).then_inc(idx_done[q], 1)
                    if z:
                        i, q = z
                        wait_reuse(dve, norm_step[q], i, 4)
                        dve.wait_ge(mv_done[q], 2 * G * i + G)
                        pass_waits(dve, passed["dve"])
                        for t in range(G):
                            dve.bn_aggr(mv[q][:, t, :], stats[q][:, t, :]).then_inc(mv_done[q], 1)
                    if bb:
                        i, q = bb
                        dve.wait_ge(idx_done[q], 2 * G * i + G)
                        pass_waits(dve, passed["dve"])
                        for t in range(G):
                            dve.max_index(idx8[q][:, t, :], top8[q][:, t, :], score[q][:, t, :])\
                                .then_inc(idx_done[q], 1)

                    def place(ks):
                        i, q = c
                        for k in ks:
                            dve.wait_ge(pos_done[q], K2 * i + k + 1)
                            dve.tensor_scalar(at_pos[q][:, k, :], slot_iota[:],
                                              rec[q][:, k:k + 1], None, ALU.is_equal)\
                                .then_inc(at_done[q], 1)

                    if c:
                        i, q = c
                        wait_reuse(dve, table_done[q], i, 1)
                        place([0])
                    if bb:
                        i, q = bb
                        dve.wait_ge(idx_done[q], 2 * G * (i + 1))
                        wait_reuse(dve, tagged_done[q], i, 2)
                        dve.tensor_tensor(onehot[q][:],
                                          idx8[q][:, :, 0:TOPK].unsqueeze(3).to_broadcast([P, G, TOPK, E]),
                                          expert_iota[:].unsqueeze(1).unsqueeze(1)
                                          .to_broadcast([P, G, TOPK, E]), ALU.is_equal).then_inc(onehot_done[q], 1)
                    if c:
                        place(range(1, K2))

                dve.wait_ge(s_const, 17)
                run_stages(dve, step, 4, NG // 2)

                dve.wait_ge(s_join, 1)
                dve.tensor_copy(token_of[:].rearrange("p e s -> p s e"),
                                psA[0][:, 0:S * E].rearrange("p (s e) -> p s e", s=S)).then_inc(tokens_done, 1)

                for q in range(2):
                    dve.wait_ge(rec_saved[q], 3 * (NG // 2))
                dve.wait_ge(s_raw[2], 16)
                fin = [0]

                def after(ins):
                    fin[0] += 1
                    ins.then_inc(s_fin, 1)
                    dve.wait_ge(s_fin, fin[0])

                for q in range(2):
                    dve.wait_ge(table_done[q], NG // 2)
                fa = work_a[1]
                total = fa[:, 0:B].rearrange("p (g t) -> p g t", t=G)
                kept = fa[:, B:3 * B].rearrange("p (g k) -> p g k", k=K2)
                scaled = fa[:, 3 * B:5 * B].rearrange("p (g k) -> p g k", k=K2)
                clipped = fa[:, 5 * B:7 * B].rearrange("p (g k) -> p g k", k=K2)
                s_of = rec_all[:, :, 0:K2].rearrange("p g (t k) -> p g t k", k=TOPK)
                pos_of = rec_all[:, :, 2 * K2:3 * K2]
                after(dve.tensor_tensor(total, s_of[:, :, :, 0], s_of[:, :, :, 1], ALU.add))
                after(dve.tensor_scalar(total, total, 1e-20, None, ALU.add))
                after(dve.reciprocal(total, total))
                after(dve.tensor_scalar(kept, pos_of, float(CAP), ROUTE_SCALE, ALU.is_lt, ALU.mult))
                after(dve.tensor_tensor(scaled, kept, rec_all[:, :, 0:K2], ALU.mult))
                sc4 = scaled.rearrange("p g (t k) -> p g t k", k=TOPK)
                for k in range(TOPK):
                    after(dve.tensor_tensor(tok_all[:, :, 1 + k, :], sc4[:, :, :, k], total, ALU.mult))
                after(dve.tensor_scalar(clipped, pos_of, float(CAP - 1), None, ALU.min))
                after(dve.scalar_tensor_tensor(slot_all[:], rec_all[:, :, K2:2 * K2], float(CAP), clipped,
                                               ALU.mult, ALU.add))
                dve.tensor_scalar(tok_all[:, :, 0, :], rec_all[:, :, 3 * K2:3 * K2 + G], bias[:, 0:1], 0.0,
                                  ALU.add, ALU.max).then_inc(fin_done, 1)
                dve.wait_ge(sw_hi_done, 2)
                dve.tensor_tensor(sw13_lo[:].rearrange("p w c s h -> p w (c s h)"), sw13_raw,
                                  sw13_hi[:].rearrange("p w c s h -> p w (c s h)").bitcast(F32),
                                  ALU.subtract).then_inc(sw_lo_done, 1)
                dve.tensor_tensor(sw2_lo[:], sw2_raw, sw2_hi[:].bitcast(F32), ALU.subtract).then_inc(sw_lo_done, 1)

                def step(a, bb, c):
                    if a:
                        i, q = a
                        wait_reuse(dve, u_done[q], i, 1)
                        for ch in range(C):
                            dve.wait_ge(rT_hi_done[q], C * i + ch + 1)
                            dve.tensor_tensor(xT_lo[q][:, ch], psT[ch][:], xT_hi[q][:, ch].bitcast(F32),
                                              ALU.subtract).then_inc(rT_lo_done[q], 1)
                    if bb:
                        i, q = bb
                        dve.wait_ge(silu_done[q], i + 1)
                        dve.wait_ge(u_done[q], i + 1)
                        wait_reuse(dve, h_hi_done[q], i, 1)
                        wait_reuse(dve, h_lo_done[q], i, 1)
                        dve.tensor_tensor(hid[q], silu[q], psGU[q][1][:], ALU.mult).then_inc(hid_done[q], 1)
                    if a:
                        i, q = a
                        dve.wait_ge(w13_hi_done[q], i + 1)
                        dve.tensor_tensor(w13_lo[q][:], w13_raw[q], w13_hi[q][:].bitcast(F32), ALU.subtract)\
                            .then_inc(w13_lo_done[q], 1)
                    if bb:
                        i, q = bb
                        wait_reuse(dve, y_done[q], i, 2)
                        dve.wait_ge(w2_hi_done[q], i + 1)
                        dve.tensor_tensor(w2_lo[q][:], w2_raw[q], w2_hi[q][:].bitcast(F32), ALU.subtract)\
                            .then_inc(w2_lo_done[q], 1)
                        dve.wait_ge(h_hi_done[q], i + 1)
                        dve.tensor_tensor(h_lo[q][:, 0], hid[q], h_hi[q][:, 0].bitcast(F32), ALU.subtract)\
                            .then_inc(h_lo_done[q], 1)
                    if c:
                        i, q = c
                        dve.wait_ge(y_done[q], 2 * (i + 1))
                        wait_reuse(dve, y_stored[q], i, 16)
                        dve.tensor_copy(y_out[q][:, 2:4, :].rearrange("p s n -> p (s n)"), psY[1][:])\
                            .then_inc(y_dve[q], 1)

                run_stages(dve, step, 3, E // 2)

                def step(a, bb, c):
                    if c:
                        i, q = c
                        dve.wait_ge(tok_set[q], i + 1)
                        for t in range(G):
                            dve.wait_ge(first_done[q], G * i + t + 1)
                            dve.scalar_tensor_tensor(pair_rows[q][:, TOPK * t, :],
                                                     pair_rows[q][:, TOPK * t + 1, :],
                                                     tok_now[q][:, 2, t:t + 1], pair_rows[q][:, TOPK * t, :],
                                                     ALU.mult, ALU.add).then_inc(two_done[q], 1)
                        dve.wait_ge(res_loaded[q], 16 * (i + 1))
                        dve.wait_ge(two_done[q], G * (i + 1))
                        dve.tensor_tensor(res[q][:], res[q][:], pair_rows[q][:, 0::TOPK, :], ALU.add)\
                            .then_inc(mix_done[q], 1)
                    if bb:
                        i, q = bb
                        wait_reuse(dve, sh_lo_done[q], i, SH)
                        wait_reuse(dve, sh_hi_done[q], i, SH)
                        for s in range(SH):
                            dve.wait_ge(ssilu_done[q], SH * i + s + 1)
                            dve.wait_ge(su_done[q], SH * i + s + 1)
                            dve.tensor_tensor(s_hid[q][:, s, :], s_silu[q][:, s, :], psS[s][1][:], ALU.mult)\
                                .then_inc(shid_done[q], 1)
                    if a:
                        i, q = a
                        wait_reuse(dve, su_done[q], i, SH)
                        dve.wait_ge(x2T_hi[q], i + 1)
                        dve.tensor_tensor(xT_lo[q][:].rearrange("p c t -> p (c t)"), x2T[q],
                                          xT_hi[q][:].rearrange("p c t -> p (c t)").bitcast(F32),
                                          ALU.subtract).then_inc(x2T_lo[q], 1)
                    if bb:
                        i, q = bb
                        wait_reuse(dve, sy_done[q], i, 2)
                        for s in range(SH):
                            dve.wait_ge(sh_hi_done[q], SH * i + s + 1)
                            dve.tensor_tensor(h_lo[q][:, s], s_hid[q][:, s, :], h_hi[q][:, s].bitcast(F32),
                                              ALU.subtract).then_inc(sh_lo_done[q], 1)
                    if c:
                        i, q = c
                        for j in range(2):
                            dve.wait_ge(sy_done[q], 2 * i + j + 1)
                            dve.wait_ge(mix_done[q], i + 1)
                            half = res[q][:, 2 * j:2 * j + 2, :].rearrange("p t n -> p (t n)")
                            dve.tensor_tensor(half, half, psY[j][:], ALU.add).then_inc(res_done[q], 1)

                for q in range(2):
                    dve.wait_ge(y_done[q], 2 * (E // 2))
                    dve.wait_ge(h_hi_done[q], E // 2)
                run_stages(dve, step, 3, NG // 2)

            @block.tensor
            def _(pe):
                pe.wait_ge(s_const, 17)
                pe.wait_ge(s_raw[0], 16)
                pe.transpose(psA[0][:, 0:P], adj_raw[:], ident[:]).then_inc(s_wT, 1)
                pe.wait_ge(s_raw[1], 16)
                for ch in range(C):
                    last = pe.transpose(psA[1][:, ch * E:(ch + 1) * E], gate_raw[:, ch::C], ident[0:E, 0:E])
                last.then_inc(s_wT, 1)
                pe.matmul(psTab[:], zero[:, 0:P], zero[:], start=True, stop=False)
                pe.wait_ge(s_wTc, 2)

                def step(z, a, bb, c):
                    if a:
                        i, q = a
                        pe.wait_ge(ln_done[q], G * (i + 1))
                        wait_before(pe, xT_done, a, C)
                        for ch in range(C):
                            for t in range(G):
                                last = pe.transpose(psT[ch][:, t * P:(t + 1) * P], xn[q][:, t, ch::C], ident[:])
                            last.then_inc(xnT_done[q], 1)
                        wait_before(pe, gmax_done, a, G // 2)

                        def neighbours(j):
                            pe.matmul(psA[j][:], adjT[:],
                                      xn[q][:, 2 * j:2 * j + 2, :].rearrange("p t n -> p (t n)"),
                                      start=True, stop=True).then_inc(gnn_done[q], 1)

                        neighbours(0)
                        pe.wait_ge(xT_done[q], C * (i + 1))
                        wait_before(pe, score_done, a, 1)
                        for t in range(G):
                            for ch in range(C):
                                last = pe.matmul(psL[:, t * E:(t + 1) * E], xT[q][:, ch, t * P:(t + 1) * P],
                                                 gateT[:, ch, :], start=(ch == 0), stop=(ch == C - 1))
                        last.then_inc(gate_done[q], 1)
                        neighbours(1)

                    def tabulate(ks):
                        i, q = c
                        for k in ks:
                            pe.wait_ge(at_done[q], K2 * i + k + 1)
                            last = pe.matmul(psTab[:], tagged[q][:, k].rearrange("p a e -> p (a e)"),
                                             at_pos[q][:, k, :], start=False, stop=False)
                        return last

                    if c:
                        pe.wait_ge(tagged_done[c[1]], 2 * (c[0] + 1))
                        tabulate(range(K2 // 2))
                    if bb:
                        i, q = bb
                        pe.wait_ge(seen_done[q], G * i + G - 1)
                        wait_before(pe, seen_done, bb, G)
                        wait_before(pe, prefix_copied, bb, 1)
                        pe.matmul(psP[:, 0:G * E], before[:], mask[q][:].rearrange("p t e -> p (t e)"),
                                  start=True, stop=False)
                        pe.matmul(psP[:, 0:G * E], ones[:], seen[q][:].rearrange("p t e -> p (t e)"),
                                  start=False, stop=True).then_inc(prefix_done[q], 1)
                    if c:
                        tabulate(range(K2 // 2, K2)).then_inc(table_done[c[1]], 1)

                run_stages(pe, step, 4, NG // 2)
                pe.matmul(psTab[:], zero[:, 0:P], zero[:], start=False, stop=True).then_inc(s_table, 1)
                pe.wait_ge(s_tabc, 1)
                for q in range(2):
                    pe.wait_ge(gmax_done[q], G // 2 * (NG // 2))
                for s in range(S):
                    last = pe.matmul(psA[0][:, s * E:(s + 1) * E], table[:, s::S], join[:],
                                     start=True, stop=True)
                last.then_inc(s_join, 1)

                def step(a, bb, c):
                    if a:
                        i, q = a
                        pe.wait_ge(gathered[q], 16 * S * (i + 1))
                        wait_before(pe, rT_hi_done, a, C)
                        wait_before(pe, rT_lo_done, a, C)
                        for ch in range(C):
                            for s in range(S):
                                last = pe.transpose(psT[ch][:, s * P:(s + 1) * P], rows[q][:, s, ch::C], ident[:])
                            last.then_inc(rowsT_done[q], 1)
                    if bb:
                        i, q = bb
                        pe.wait_ge(w13_hi_done[q], i + 1)
                        pe.wait_ge(w13_lo_done[q], i + 1)
                        pe.wait_ge(rT_hi_done[q], C * (i + 1))
                        pe.wait_ge(rT_lo_done[q], C * (i + 1))
                        wait_reuse(pe, silu_done[q], i, 1)
                        wait_reuse(pe, hid_done[q], i, 1)
                        for k, done in enumerate((g_done, u_done)):
                            three_passes(pe, psGU[q][k][:], [
                                ((w13_hi[q][:, k, ch], w13_lo[q][:, k, ch]), (xT_hi[q][:, ch], xT_lo[q][:, ch]))
                                for ch in range(C)]).then_inc(done[q], 1)
                    if c:
                        i, q = c
                        pe.wait_ge(w2_hi_done[q], i + 1)
                        pe.wait_ge(w2_lo_done[q], i + 1)
                        pe.wait_ge(h_hi_done[q], i + 1)
                        pe.wait_ge(h_lo_done[q], i + 1)
                        wait_before(pe, y_act, c, 1)
                        wait_before(pe, y_dve, c, 1)
                        for j in range(2):
                            for s in (2 * j, 2 * j + 1):
                                last = three_passes(pe, psY[j][:, s % 2 * N:(s % 2 + 1) * N], [
                                    ((h_hi[q][:, 0, s * P:(s + 1) * P], h_lo[q][:, 0, s * P:(s + 1) * P]),
                                     (w2_hi[q][:], w2_lo[q][:]))])
                            last.then_inc(y_done[q], 1)

                run_stages(pe, step, 3, E // 2)

                def step(a, bb, c):
                    if bb:
                        i, q = bb
                        pe.wait_ge(x2T_hi[q], i + 1)
                        pe.wait_ge(x2T_lo[q], i + 1)
                        wait_before(pe, ssilu_done, bb, SH)
                        wait_before(pe, shid_done, bb, SH)
                        for s in range(SH):
                            for k, done in enumerate((sg_done, su_done)):
                                three_passes(pe, psS[s][k][:], [
                                    ((sw13_hi[:, k, ch, s], sw13_lo[:, k, ch, s]),
                                     (xT_hi[q][:, ch], xT_lo[q][:, ch])) for ch in range(C)]).then_inc(done[q], 1)
                    if c:
                        i, q = c
                        pe.wait_ge(sh_hi_done[q], SH * (i + 1))
                        pe.wait_ge(sh_lo_done[q], SH * (i + 1))
                        wait_before(pe, res_done, c, 2)
                        for j in range(2):
                            for t in (2 * j, 2 * j + 1):
                                last = three_passes(pe, psY[j][:, t % 2 * N:(t % 2 + 1) * N], [
                                    ((h_hi[q][:, s, t * P:(t + 1) * P], h_lo[q][:, s, t * P:(t + 1) * P]),
                                     (sw2_hi[:, s], sw2_lo[:, s])) for s in range(SH)])
                            last.then_inc(sy_done[q], 1)

                pe.wait_ge(sw_lo_done, 2)
                for q in range(2):
                    pe.wait_ge(hid_done[q], E // 2)
                    pe.wait_ge(y_act[q], E // 2)
                    pe.wait_ge(y_dve[q], E // 2)
                run_stages(pe, step, 3, NG // 2)


_INS = ['x', 'adj', 'L0_gnn_b', 'L0_ffn_gate_w', 'L0_ffn_w1', 'L0_ffn_w3', 'L0_ffn_w2', 'L0_ffn_sw1', 'L0_ffn_sw3',
        'L0_ffn_sw2']
_OUTS = [((128, 128, 256), 'float32')]


def kernel(**inputs):
    import numpy as _np
    import concourse.bacc as _bacc
    from concourse import mybir as _mybir
    from concourse.bass_utils import run_bass_kernel_spmd as _run

    nc = _bacc.Bacc("TRN2", target_bir_lowering=False, num_devices=1)
    arrays, args = {}, []
    for name in _INS:
        a = _np.ascontiguousarray(inputs[name])
        arrays[f"in_{name}_dram"] = a
        args.append(nc.dram_tensor(f"in_{name}_dram", a.shape, _mybir.dt.from_np(a.dtype), kind="ExternalInput").ap())
    for i, (shape, dtype) in enumerate(_OUTS):
        dt = _mybir.dt.from_np(_np.dtype(dtype))
        args.append(nc.dram_tensor(f"out_{i}_dram", shape, dt, kind="ExternalOutput").ap())
    build(nc, *args)
    r = _run(nc, [arrays], core_ids=[0])
    return r.results[0]["out_0_dram"]
```
